# Optimizing a Trainium2 kernel written in Bass

```python
import numpy as np
import jax
import jax.numpy as jnp

def _softmax(x, axis=-1):
    return jax.nn.softmax(x, axis=axis)

def _gelu(x):
    return jax.nn.gelu(x, approximate=True)

def _silu(x):
    return jax.nn.silu(x)

def _sigmoid(x):
    return jax.nn.sigmoid(x)

def _layernorm(x, axis=-1, eps=1e-05):
    m = jnp.mean(x, axis=axis, keepdims=True)
    v = jnp.var(x, axis=axis, keepdims=True)
    return (x - m) / jnp.sqrt(v + eps)

def _scatter_add(tgt, idx, src, axis=0):
    return tgt.at[idx].add(src)

def _segment_sum(src, seg, n):
    return jax.ops.segment_sum(src, seg, n)
kernel_name = 'mk_gnn_preln_d2_gnn_r8_0da2e2'

def setup_inputs(seed: int=0):
    np.random.seed(seed)
    _w = jnp.asarray

    def _rec_inputs():
        import jax
        import jax.numpy as jnp
        _gk = jax.random.key(seed)
        x = 8.953e-05 + 1 * jax.random.normal(jax.random.fold_in(_gk, 1), (12500, 32), jnp.float32)
        src = jax.random.randint(jax.random.fold_in(_gk, 2), (200000,), 0, 12500, jnp.int32)
        dst = jax.random.randint(jax.random.fold_in(_gk, 3), (200000,), 0, 12500, jnp.int32)
        _o = jnp.argsort(dst, stable=True)
        src = src[_o]
        dst = dst[_o]
        edge_attr_3 = jax.random.uniform(jax.random.fold_in(_gk, 12), (200000, 3), jnp.float32, 0.0, 0.999998)
        return (x, src, dst, edge_attr_3)
    x, src, dst, edge_attr_3 = _rec_inputs()

    def _L0_gnn_setup():
        import jax, jax.numpy as jnp
        import numpy as np
        D = 3
        KS = 5
        K = KS ** D
        S = 2 ** D
        _COMBOS = np.array([[s >> d & 1 for d in range(D)] for s in range(S)], dtype=np.int32)
        _STRIDES = np.array([KS ** (D - 1 - d) for d in range(D)], dtype=np.int32)

        def spline_basis(pseudo):
            pos = pseudo * (KS - 1)
            i0 = jnp.clip(jnp.floor(pos), 0, KS - 2).astype(jnp.int32)
            frac = pos - i0
            combos = jnp.asarray(_COMBOS)
            basis = jnp.prod(jnp.where(combos[None] == 1, frac[:, None, :], 1.0 - frac[:, None, :]), axis=-1)
            idx = jnp.sum((i0[:, None, :] + combos[None]) * jnp.asarray(_STRIDES)[None, None, :], axis=-1)
            return (basis, idx)

        def spline_conv(x, row, col, basis, idx, W, b):
            N = x.shape[0]
            Fout = W.shape[2]
            z = jnp.einsum('ni,kio->nko', x, W).reshape(N * K, Fout)
            gathered = z[col[:, None] * K + idx]
            msg = jnp.einsum('es,eso->eo', basis, gathered)
            out = jax.ops.segment_sum(msg, row, num_segments=N)
            deg = jax.ops.segment_sum(jnp.ones_like(msg[:, 0]), row, num_segments=N)
            return out / jnp.maximum(deg, 1.0)[:, None] + b
        key = jax.random.key(seed)
        ks = jax.random.split(key, 13)
        N, E, Fin, Fout = (2500, 40000, 32, 32)

        def u(k, shape, size):
            bound = 1.0 / np.sqrt(size)
            return jax.random.uniform(k, shape, jnp.float32, -bound, bound)
        return dict(x=jax.random.normal(ks[0], (N, Fin), jnp.float32), edge_index=jax.random.randint(ks[1], (2, E), 0, N, dtype=jnp.int32), pseudo=jax.random.uniform(ks[2], (E, D), jnp.float32), stn1_w=u(ks[3], (K, 1, 64), 1 * S), stn1_b=u(ks[4], (64,), 1 * S), stn2_w=u(ks[5], (K, 64, 64), 64 * S), stn2_b=u(ks[6], (64,), 64 * S), stn3_w=u(ks[7], (64, 64), 64), stn3_b=u(ks[8], (64,), 64), stn4_w=u(ks[9], (64, 3), 64), stn4_b=u(ks[10], (3,), 64), conv_w=u(ks[11], (K, Fin, Fout), Fin * S), conv_b=u(ks[12], (Fout,), Fin * S))
    _L0_gnn_all = _L0_gnn_setup()
    _L0_gnn_in = {k: v for k, v in _L0_gnn_all.items() if k in ('stn1_w', 'stn1_b', 'stn2_w', 'stn2_b', 'stn3_w', 'stn3_b', 'stn4_w', 'stn4_b', 'conv_w', 'conv_b')}
    del _L0_gnn_all

    def _L1_gnn_setup():
        import jax, jax.numpy as jnp
        import numpy as np
        N_NODES = 6250
        N_EDGES = 100000
        IN_FEATS = 32
        OUT_FEATS = 32
        NUM_HEADS = 4
        key = jax.random.key(seed)
        ks = jax.random.split(key, 12)
        H, F, IN = (NUM_HEADS, OUT_FEATS, IN_FEATS)
        h = jax.random.normal(ks[0], (N_NODES, IN), dtype=jnp.float32)
        src = jax.random.randint(ks[1], (N_EDGES,), 0, N_NODES, dtype=jnp.int64)
        dst = jax.random.randint(ks[2], (N_EDGES,), 0, N_NODES, dtype=jnp.int64)
        s = 0.1
        W_gat = jax.random.normal(ks[3], (IN, H * F), dtype=jnp.float32) * s
        attn_l = jax.random.normal(ks[4], (H, F), dtype=jnp.float32) * s
        attn_r = jax.random.normal(ks[5], (H, F), dtype=jnp.float32) * s
        W_ih = jax.random.normal(ks[6], (3 * F, H * F), dtype=jnp.float32) * s
        W_hh = jax.random.normal(ks[7], (3 * F, F), dtype=jnp.float32) * s
        b_ih = jax.random.normal(ks[8], (3 * F,), dtype=jnp.float32) * s
        b_hh = jax.random.normal(ks[9], (3 * F,), dtype=jnp.float32) * s
        return {'h': h, 'W_gat': W_gat, 'attn_l': attn_l, 'attn_r': attn_r, 'W_ih': W_ih, 'W_hh': W_hh, 'b_ih': b_ih, 'b_hh': b_hh, 'src': src, 'dst': dst}
    _L1_gnn_all = _L1_gnn_setup()
    _L1_gnn_in = {k: v for k, v in _L1_gnn_all.items() if k in ('W_gat', 'attn_l', 'attn_r', 'W_ih', 'W_hh', 'b_ih', 'b_hh')}
    del _L1_gnn_all
    return {'x': x, 'src': src, 'dst': dst, 'edge_attr_3': edge_attr_3, 'L0_gnn_stn1_w': _L0_gnn_in['stn1_w'], 'L0_gnn_stn1_b': _L0_gnn_in['stn1_b'], 'L0_gnn_stn2_w': _L0_gnn_in['stn2_w'], 'L0_gnn_stn2_b': _L0_gnn_in['stn2_b'], 'L0_gnn_stn3_w': _L0_gnn_in['stn3_w'], 'L0_gnn_stn3_b': _L0_gnn_in['stn3_b'], 'L0_gnn_stn4_w': _L0_gnn_in['stn4_w'], 'L0_gnn_stn4_b': _L0_gnn_in['stn4_b'], 'L0_gnn_conv_w': _L0_gnn_in['conv_w'], 'L0_gnn_conv_b': _L0_gnn_in['conv_b'], 'L1_gnn_W_gat': _L1_gnn_in['W_gat'], 'L1_gnn_attn_l': _L1_gnn_in['attn_l'], 'L1_gnn_attn_r': _L1_gnn_in['attn_r'], 'L1_gnn_W_ih': _L1_gnn_in['W_ih'], 'L1_gnn_W_hh': _L1_gnn_in['W_hh'], 'L1_gnn_b_ih': _L1_gnn_in['b_ih'], 'L1_gnn_b_hh': _L1_gnn_in['b_hh']}

def reference(x, src, dst, edge_attr_3, L0_gnn_stn1_w, L0_gnn_stn1_b, L0_gnn_stn2_w, L0_gnn_stn2_b, L0_gnn_stn3_w, L0_gnn_stn3_b, L0_gnn_stn4_w, L0_gnn_stn4_b, L0_gnn_conv_w, L0_gnn_conv_b, L1_gnn_W_gat, L1_gnn_attn_l, L1_gnn_attn_r, L1_gnn_W_ih, L1_gnn_W_hh, L1_gnn_b_ih, L1_gnn_b_hh):
    import jax
    import jax.numpy as jnp

    def _L0_gnn_ref(x, edge_index, pseudo, stn1_w, stn1_b, stn2_w, stn2_b, stn3_w, stn3_b, stn4_w, stn4_b, conv_w, conv_b):
        import jax, jax.numpy as jnp
        import numpy as np
        D = 3
        KS = 5
        K = KS ** D
        S = 2 ** D
        _COMBOS = np.array([[s >> d & 1 for d in range(D)] for s in range(S)], dtype=np.int32)
        _STRIDES = np.array([KS ** (D - 1 - d) for d in range(D)], dtype=np.int32)

        def spline_basis(pseudo):
            pos = pseudo * (KS - 1)
            i0 = jnp.clip(jnp.floor(pos), 0, KS - 2).astype(jnp.int32)
            frac = pos - i0
            combos = jnp.asarray(_COMBOS)
            basis = jnp.prod(jnp.where(combos[None] == 1, frac[:, None, :], 1.0 - frac[:, None, :]), axis=-1)
            idx = jnp.sum((i0[:, None, :] + combos[None]) * jnp.asarray(_STRIDES)[None, None, :], axis=-1)
            return (basis, idx)

        def spline_conv(x, row, col, basis, idx, W, b):
            N = x.shape[0]
            Fout = W.shape[2]
            z = jnp.einsum('ni,kio->nko', x, W).reshape(N * K, Fout)
            gathered = z[col[:, None] * K + idx]
            msg = jnp.einsum('es,eso->eo', basis, gathered)
            out = jax.ops.segment_sum(msg, row, num_segments=N)
            deg = jax.ops.segment_sum(jnp.ones_like(msg[:, 0]), row, num_segments=N)
            return out / jnp.maximum(deg, 1.0)[:, None] + b
        N = x.shape[0]
        row, col = (edge_index[0], edge_index[1])
        basis, idx = spline_basis(pseudo)
        h = jnp.ones((N, 1), x.dtype)
        h = jax.nn.elu(spline_conv(h, row, col, basis, idx, stn1_w, stn1_b))
        h = jax.nn.elu(spline_conv(h, row, col, basis, idx, stn2_w, stn2_b))
        h = jax.nn.elu(h @ stn3_w + stn3_b)
        t = h @ stn4_w + stn4_b
        new_pseudo = jnp.clip(pseudo + t[col] - t[row], 0.0, 1.0)
        basis2, idx2 = spline_basis(new_pseudo)
        return spline_conv(x, row, col, basis2, idx2, conv_w, conv_b)

    def _L1_gnn_ref(h, W_gat, attn_l, attn_r, W_ih, W_hh, b_ih, b_hh, src, dst):
        import jax, jax.numpy as jnp
        import numpy as np
        N_NODES = 6250
        N_EDGES = 100000
        IN_FEATS = 32
        OUT_FEATS = 32
        NUM_HEADS = 4
        N = h.shape[0]
        H, F = attn_l.shape
        feat = (h @ W_gat).reshape(N, H, F)
        el = jnp.einsum('nhf,hf->nh', feat, attn_l)
        er = jnp.einsum('nhf,hf->nh', feat, attn_r)
        e = jax.nn.leaky_relu(el[src] + er[dst], 0.2)
        emax = jax.ops.segment_max(e, dst, num_segments=N)
        ee = jnp.exp(e - emax[dst])
        denom = jax.ops.segment_sum(ee, dst, num_segments=N)
        alpha = ee / denom[dst]
        msg = feat[src] * alpha[:, :, None]
        agg = jax.ops.segment_sum(msg, dst, num_segments=N)
        x = agg.reshape(N, H * F)
        gi = x @ W_ih.T + b_ih
        gh = h @ W_hh.T + b_hh
        i_r, i_z, i_n = jnp.split(gi, 3, axis=1)
        h_r, h_z, h_n = jnp.split(gh, 3, axis=1)
        r = jax.nn.sigmoid(i_r + h_r)
        z = jax.nn.sigmoid(i_z + h_z)
        n = jnp.tanh(i_n + r * h_n)
        h_new = (1.0 - z) * n + z * h
        return jax.nn.elu(h_new)
    edge_index = jnp.stack([src, dst])
    h = jnp.maximum(_layernorm(x, axis=-1), 0.0)
    x = x + _L0_gnn_ref(h, edge_index, edge_attr_3, L0_gnn_stn1_w, L0_gnn_stn1_b, L0_gnn_stn2_w, L0_gnn_stn2_b, L0_gnn_stn3_w, L0_gnn_stn3_b, L0_gnn_stn4_w, L0_gnn_stn4_b, L0_gnn_conv_w, L0_gnn_conv_b)
    h = jnp.maximum(_layernorm(x, axis=-1), 0.0)
    x = x + _L1_gnn_ref(h, L1_gnn_W_gat, L1_gnn_attn_l, L1_gnn_attn_r, L1_gnn_W_ih, L1_gnn_W_hh, L1_gnn_b_ih, L1_gnn_b_hh, src, dst)
    return x

_drawn_inputs = setup_inputs


def setup_inputs(seed=0):
    import zlib

    import numpy as np

    out = dict(_drawn_inputs(seed))
    spreads = {}
    factors = {'edge_attr_3': 2.851,
     'L0_gnn_stn1_w': 8.0,
     'L0_gnn_stn1_b': 154.662,
     'L0_gnn_stn2_w': 8.0,
     'L0_gnn_stn2_b': 200.0,
     'L0_gnn_stn3_w': 8.0,
     'L0_gnn_stn3_b': 200.0,
     'L0_gnn_stn4_w': 8.0,
     'L0_gnn_stn4_b': 8.0,
     'L1_gnn_attn_l': 8.0,
     'L1_gnn_attn_r': 24.541,
     'L1_gnn_b_hh': 2.714}
    for name, (base, spread) in spreads.items():
        noise = np.random.default_rng([zlib.crc32(name.encode()), seed]).standard_normal(out[name].shape)
        drawn = base * np.exp(spread * noise) if base else spread * noise
        out[name] = jnp.asarray(drawn.astype(out[name].dtype))
    for name, factor in factors.items():
        out[name] = (out[name] * factor).astype(out[name].dtype)
    return out
```

```python
from contextlib import ExitStack

import concourse.bass as bass
from concourse import mybir

F32 = mybir.dt.float32
BF16 = mybir.dt.bfloat16
I32 = mybir.dt.int32
U32 = mybir.dt.uint32
ALU = mybir.AluOpType
ACT = mybir.ActivationFunctionType
X = mybir.AxisListType.X

P = 128
N = 12500
E = 200000
NB = -(-N // P)
NP = NB * P
NT = 1568
EP = P * NT
LAST = E - (P - 1) * NT
G = 8
NG = NT // G
WN = 4
NW = P // WN
NQ = NW // G
SPREADS = 4
ROW = 8
EPS = 1e-5
FEAT = 32
HID = 64
K = 125
HEADS = 4
BIG = 1e30
SLOPE = 0.2


def bc(ap, shape):
    return ap.to_broadcast(shape)


class Chain:

    def __init__(self, eng, sem):
        self.eng, self.sem, self.n = eng, sem, 0

    def __call__(self, ins):
        self.n += 1
        ins.then_inc(self.sem, 1)
        self.eng.wait_ge(self.sem, self.n)


def allocators(nc, ctx):
    def sb(name, shape, dt=F32):
        return ctx.enter_context(nc.sbuf_tensor(name, shape, dt))

    def ps(name, shape, dt=F32):
        return ctx.enter_context(nc.psum_tensor(name, shape, dt))

    def sem(name):
        return ctx.enter_context(nc.semaphore(name))

    return sb, ps, sem


def constants(nc, c, d, sem):
    ready, chain_sem = sem("const_iota"), sem("const_chain")
    with nc.Block() as block:
        @block.gpsimd
        def _(pool):
            pool.iota(c.ramp_i[:, :], pattern=[[1, P]], base=0, channel_multiplier=0).then_inc(ready, 1)
            pool.iota(c.part_i[:, :], pattern=[[0, 1]], base=0, channel_multiplier=1).then_inc(ready, 1)

        @block.vector
        def _(dve):
            chain = Chain(dve, chain_sem)
            dve.wait_ge(ready, 2)
            chain(dve.tensor_copy(c.ramp[:, :], c.ramp_i[:, :]))
            chain(dve.tensor_copy(c.part[:, :], c.part_i[:, :]))
            chain(dve.tensor_copy(c.ramp_bf[:, :], c.ramp[:, :]))
            chain(dve.tensor_scalar(c.ident[:, :], c.ramp[:, :], c.part[:, 0:1], None, ALU.is_equal))
            chain(dve.tensor_copy(c.ident_bf[:, :], c.ident[:, :]))
            chain(dve.tensor_scalar(c.before[:, :], c.ramp[:, :], c.part[:, 0:1], None, ALU.is_lt))
            chain(dve.tensor_scalar(c.after[:, :], c.ramp[:, :], c.part[:, 0:1], None, ALU.is_gt))
            chain(dve.memset(c.ones[:, :], 1.0))
            chain(dve.tensor_copy(c.window_ramp[:, :, :, :].rearrange("p q g r -> p (q g r)"), c.ramp[:, :]))
            chain(dve.tensor_scalar(c.first[:, :], c.ramp[:, 0:NB], float(P), None, ALU.mult))
            chain(dve.tensor_scalar(c.jm[:, :], c.ramp[:, 0:5], -1.0, None, ALU.add))
            chain(dve.tensor_scalar(c.jp[:, :], c.ramp[:, 0:5], 1.0, None, ALU.add))
            chain(dve.memset(c.up_floor[:, :], 0.0))
            chain(dve.memset(c.up_floor[:, 0:1], BIG))
            chain(dve.memset(c.up_floor[:, 1:2], -BIG))
            chain(dve.memset(c.down_floor[:, :], 0.0))
            chain(dve.memset(c.down_floor[:, 3:4], -BIG))
            chain(dve.memset(c.down_floor[:, 4:5], BIG))
            chain(dve.memset(c.zeros[:, :], 0.0))


def layer_norm_relu(dve, chain, act_turn, act_done, turn, out, x, tmp, stat):
    shape = [P, NB, FEAT]
    mean, var, rstd = stat[:, 0, :], stat[:, 1, :], stat[:, 2, :]
    chain(dve.tensor_reduce(mean, x, X, ALU.add))
    chain(dve.tensor_scalar(mean, mean, 1.0 / FEAT, None, ALU.mult))
    chain(dve.tensor_tensor(out, x, bc(mean.unsqueeze(2), shape), ALU.subtract))
    chain(dve.tensor_tensor(tmp, out, out, ALU.mult))
    chain(dve.tensor_reduce(var, tmp, X, ALU.add))
    chain(dve.tensor_scalar(var, var, 1.0 / FEAT, EPS, ALU.mult, ALU.add))
    dve.sem_inc(act_turn, 1)
    dve.wait_ge(act_done, turn)
    chain(dve.reciprocal(rstd, rstd))
    chain(dve.tensor_tensor(out, out, bc(rstd.unsqueeze(2), shape), ALU.mult))
    chain(dve.tensor_scalar(out, out, 0.0, None, ALU.max))


def node_view(dram, f):
    return dram.rearrange("(b p) f -> p b f", p=P)


def load_nodes_and_edges(nc, c, d, sem):
    cleared, loaded, chain_sem, var_ready, std_ready = (
        sem("in_cleared"), sem("in_loaded"), sem("in_chain"), sem("in_var"), sem("in_std"))
    full = (N // P) * P
    with nc.Block() as block, ExitStack() as ctx:
        sb, _, _ = allocators(nc, ctx)
        tmp, stat = sb("ln_tmp", [P, NB, FEAT]), sb("ln_stat", [P, 3, NB])
        pseudo = sb("pseudo", [P, NT, 3])
        rec_dst = sb("rec_dst_sb", [P, NT, 2])
        dst_made, dst_stored = sem("in_dst_made"), sem("in_dst_stored")

        @block.sync
        def _(sp):
            sp.wait_ge(cleared, 1)
            sp.dma_start(c.x[:, 0:N // P, :], d.x[0:full, :].rearrange("(b p) f -> p b f", p=P)).then_inc(loaded, 16)
            sp.dma_start(c.x[0:N - full, NB - 1, :], d.x[full:N, :]).then_inc(loaded, 16)
            for a, n in ((c.src_i, d.src), (c.dst_i, d.dst)):
                sp.dma_start(a[0:P - 1, :], n[0:(P - 1) * NT].rearrange("(p t) -> p t", t=NT)).then_inc(loaded, 16)
                sp.dma_start(a[P - 1:P, 0:LAST], n[(P - 1) * NT:E].rearrange("(p t) -> p t", p=1)).then_inc(loaded, 16)
            sp.dma_start(pseudo[0:P - 1, :, :],
                         d.attr[0:(P - 1) * NT, :].rearrange("(p t) k -> p t k", t=NT)).then_inc(loaded, 16)
            sp.dma_start(pseudo[P - 1:P, 0:LAST, :],
                         d.attr[(P - 1) * NT:E, :].rearrange("(p t) k -> p t k", p=1)).then_inc(loaded, 16)
            sp.wait_ge(dst_made, 1)
            sp.dma_start(d.rec_dst.rearrange("(p t) w -> p t w", t=NT), rec_dst[:, :, :]).then_inc(dst_stored, 16)
            sp.wait_ge(dst_stored, 16)

        @block.scalar
        def _(act):
            act.wait_ge(var_ready, 1)
            act.activation(stat[:, 2, :], stat[:, 1, :], ACT.Sqrt).then_inc(std_ready, 1)

        @block.vector
        def _(dve):
            chain = Chain(dve, chain_sem)
            chain(dve.memset(c.x[:, :, :], 0.0))
            chain(dve.memset(c.src_i[:, :], NP - 1))
            chain(dve.memset(c.dst_i[:, :], NP - 1))
            for a in (c.src, c.src_lo, c.src_hi):
                chain(dve.memset(a[:, NT:NT + G], 0.0))
            chain(dve.memset(pseudo[:, :, :], 0.0))
            chain(dve.memset(c.rec[:, :, :], 0.0))
            dve.sem_inc(cleared, 1)
            dve.wait_ge(loaded, 16 * 8)
            for key_i, key, lo, hi in ((c.src_i, c.src, c.src_lo, c.src_hi), (c.dst_i, None, c.dst_lo, c.dst_hi)):
                if key is not None:
                    chain(dve.tensor_copy(key[:, 0:NT], key_i[:, :]))
                chain(dve.tensor_scalar(c.key_tmp[:, :], key_i[:, :], P - 1, None, ALU.bitwise_and))
                chain(dve.tensor_copy(lo[:, 0:NT], c.key_tmp[:, :]))
                chain(dve.tensor_scalar(c.key_tmp[:, :], key_i[:, :], 7, None, ALU.logical_shift_right))
                chain(dve.tensor_copy(hi[:, 0:NT], c.key_tmp[:, :]))
            chain(dve.tensor_copy(c.rec[:, :, 0:1], c.src[:, 0:NT].unsqueeze(2)))
            chain(dve.tensor_copy(c.rec[:, :, 1:2].bitcast(I32), c.dst_i[:, :].unsqueeze(2)))
            chain(dve.tensor_copy(c.rec[:, :, 2:5], pseudo[:, :, :]))
            chain(dve.tensor_copy(rec_dst[:, :, 0:1].bitcast(I32), c.src_i[:, :].unsqueeze(2)))
            chain(dve.tensor_copy(rec_dst[:, :, 1:2], c.dst_i[:, :].unsqueeze(2)))
            dve.sem_inc(dst_made, 1)
            layer_norm_relu(dve, chain, var_ready, std_ready, 1, c.h[:, :, :], c.x[:, :, :], tmp[:, :, :], stat)


def count_and_prefix(nc, c, d, sem):
    free = sem("cnt_free")
    made = sem("cnt_made")
    counted, chain_sem, pe_ready, pe_chain = sem("cnt_done"), sem("cnt_chain"), sem("cnt_pe"), sem("cnt_pe_turn")
    stored, act_c = sem("cnt_stored"), sem("cnt_sorted")
    with nc.Block() as block, ExitStack() as ctx:
        sb, ps, _ = allocators(nc, ctx)
        lo_hot = [sb(f"cnt_lo{k}", [P, 2, G, P], BF16) for k in range(2)]
        hi_hot = [sb(f"cnt_hi{k}", [P, 2, G, NB], BF16) for k in range(2)]
        count = [ps(f"cnt_ps{k}", [P, 512]) for k in range(2)]
        total = ps("cnt_total", [P, 512])
        within = ps("cnt_within", [P, 512])
        turned = ps("cnt_turned", [P, 512])
        off = sb("cnt_off", [NB, 2, NW], I32)
        starts = [sb(f"cnt_starts{k}", [1, NB * NW], I32) for k in range(2)]
        tot_sb = sb("cnt_tot", [P, 2, NB])
        fill, fullest, full_i = sb("cnt_fill", [1, NB * NW]), sb("cnt_fullest", [1, 2]), sb("cnt_full_i", [1, 1], I32)

        @block.vector
        def _(dve):
            with dve.Fori(0, NG // 2) as i:
                for u in range(2):
                    dve.wait_ge(free, i * 2 + u + 1)
                    for k, (lo, hi) in enumerate(((c.src_lo, c.src_hi), (c.dst_lo, c.dst_hi))):
                        at = bass.ds((i * 2 + u) * G, G)
                        dve.tensor_tensor(lo_hot[k][:, u, :, :], bc(c.ramp_bf[:, :].unsqueeze(1), [P, G, P]),
                                          bc(lo[:, at].unsqueeze(2), [P, G, P]), ALU.is_equal).then_inc(made, 1)
                        dve.tensor_tensor(hi_hot[k][:, u, :, :], bc(c.ramp_bf[:, 0:NB].unsqueeze(1), [P, G, NB]),
                                          bc(hi[:, at].unsqueeze(2), [P, G, NB]), ALU.is_equal).then_inc(made, 1)
            chain = Chain(dve, chain_sem)
            dve.wait_ge(counted, 1)
            chain(dve.tensor_copy(c.deg[:, :], count[0][:, 0:NB]))
            chain(dve.tensor_copy(c.base[:, 1, :], count[1][:, 0:NB]))
            dve.sem_inc(pe_ready, 1)
            dve.wait_ge(counted, 2)
            for k, cnt in enumerate((c.deg[:, :], c.base[:, 1, :])):
                chain(dve.tensor_copy(tot_sb[:, k, :], total[:, k * P:k * P + NB]))
                chain(dve.tensor_tensor_scan(c.scan[:, :], bc(c.ones[:, 0:1], [P, NB]), tot_sb[:, k, :], 0.0,
                                             ALU.mult, ALU.add))
                chain(dve.tensor_tensor(c.scan[:, :], c.scan[:, :], tot_sb[:, k, :], ALU.subtract))
                chain(dve.tensor_tensor(c.base[:, k, :], c.scan[:, :], within[:, k * P:k * P + NB], ALU.add))
            dve.sem_inc(pe_ready, 1)
            dve.wait_ge(counted, 3)
            for k in range(2):
                first = turned[0:NB, k * P:(k + 1) * P].rearrange("p (w n) -> p w n", n=WN)[:, :, 0]
                chain(dve.tensor_copy(off[:, k, :], first))
            dve.sem_inc(pe_ready, 1)
            dve.wait_ge(act_c, 1)
            for k in range(2):
                last = N // WN
                chain(dve.tensor_tensor(fill[:, 0:last], starts[k][:, 1:last + 1], starts[k][:, 0:last], ALU.subtract))
                chain(dve.tensor_reduce(fullest[:, 0:1], fill[:, 0:last], X, ALU.max))
                chain(dve.tensor_scalar(fullest[:, 1:2], fullest[:, 0:1], float(P - 1), float(P), ALU.add, ALU.max))
                chain(dve.tensor_copy(full_i[:, :], fullest[:, 1:2]))
                chain(dve.tensor_scalar(c.pass_count[:, k:k + 1], full_i[:, :], 7, None, ALU.logical_shift_right))

        @block.tensor
        def _(pe):
            for k in range(2):
                pe.matmul(count[k][:, 0:NB], c.zeros[:, 0:P], c.zeros[:, 0:NB], start=True, stop=False)\
                    .then_inc(free, 1)
            with pe.Fori(0, NG // 2) as i:
                for u in range(2):
                    pe.wait_ge(made, i * 8 + u * 4 + 4)
                    for k in range(2):
                        for j in range(G):
                            last = pe.matmul(count[k][:, 0:NB], lo_hot[k][:, u, j, :], hi_hot[k][:, u, j, :],
                                             start=False, stop=False, skip_group_check=True)
                    last.then_inc(free, 1)
            for k in range(2):
                last = pe.matmul(count[k][:, 0:NB], c.zeros[:, 0:P], c.zeros[:, 0:NB], start=False, stop=True)
            last.then_inc(counted, 1)
            pe.wait_ge(pe_ready, 1)
            for k, cnt in enumerate((c.deg[:, :], c.base[:, 1, :])):
                pe.matmul(total[:, k * P:k * P + NB], c.ones[:, :], cnt, start=True, stop=True)
                last = pe.matmul(within[:, k * P:k * P + NB], c.after[:, :], cnt, start=True, stop=True)
            last.then_inc(counted, 1)
            pe.wait_ge(pe_ready, 2)
            for k in range(2):
                last = pe.transpose(turned[0:NB, k * P:(k + 1) * P], c.base[:, k, :], c.ident[:, :])
            last.then_inc(counted, 1)

        @block.sync
        def _(sp):
            sp.wait_ge(pe_ready, 3)
            for k in range(2):
                sp.dma_start(d.off[k].rearrange("(b w) -> b w", w=NW), off[:, k, :]).then_inc(stored, 16)
            sp.wait_ge(stored, 32)
            for k in range(2):
                sp.dma_start(starts[k][0:1, :], d.off[k].rearrange("(a w) -> a w", a=1)).then_inc(stored, 16)
            sp.wait_ge(stored, 64)
            sp.sem_inc(act_c, 1)


def sort_edges(nc, c, d, sem):
    hots_made = sem("rk_hots_made")
    turned = sem("rk_turned")
    lo_ready = sem("rk_lo_ready")
    cols_made = sem("rk_cols_made")
    rows_made = sem("rk_rows_made")
    looked = sem("rk_looked")
    updated = sem("rk_updated")
    table_ready = sem("rk_table_ready")
    sums = sem("rk_sums")
    place_made = sem("rk_place_made")
    rec_ready = sem("rk_rec_ready")
    scattered = c.scattered
    pool_turn = sem("rk_pool_turn")
    tail_made = sem("rk_tail_made")
    with nc.Block() as block, ExitStack() as ctx:
        sb, ps, _ = allocators(nc, ctx)
        lo_hot, hi_hot = sb("rk_lo", [P, 2, G, P], BF16), sb("rk_hi", [P, 2, G, NB], BF16)
        lo_t = sb("rk_lo_t", [P, 2, G, P])
        table = sb("rk_table", [P, 2, NB])
        junk, junk_l = sb("rk_junk", [P, 2, G, P], BF16), sb("rk_junk_l", [P, 2, G, NB], BF16)
        in_tile, before = sb("rk_in_tile", [P, 2, G]), sb("rk_before", [P, 2, G])
        place = sb("rk_place", [P, 2, G], U32)
        rec = sb("rk_rec", [P, 2, G, ROW])
        cols = sb("rk_cols", [P, 2, G])
        tail = sb("rk_tail", [P, 2, ROW])
        lo_ps = ps("rk_lo_ps", [P, G, P], BF16)
        rows = ps("rk_rows_ps", [P, 2, G, P])
        look = ps("rk_look_ps", [P, 2, 512])
        run = ps("rk_run_ps", [P, 512])

        @block.vector
        def _(dve):
            def hots(g, u):
                at = bass.ds(g * G, G)
                dve.tensor_tensor(lo_hot[:, u, :, :], bc(c.ramp_bf[:, :].unsqueeze(1), [P, G, P]),
                                  bc(c.src_lo[:, at].unsqueeze(2), [P, G, P]), ALU.is_equal).then_inc(hots_made, 1)
                dve.tensor_tensor(hi_hot[:, u, :, :], bc(c.ramp_bf[:, 0:NB].unsqueeze(1), [P, G, NB]),
                                  bc(c.src_hi[:, at].unsqueeze(2), [P, G, NB]), ALU.is_equal).then_inc(hots_made, 1)

            dve.memset(tail[:, :, :], -1.0).then_inc(tail_made, 1)
            dve.sem_inc(sums, 4)
            dve.sem_inc(place_made, 2)
            hots(0, 0)
            with dve.Fori(0, NG // 2) as i:
                for u in range(2):
                    g = i * 2 + u
                    dve.wait_ge(updated, g * G + 1)
                    hots(g + 1, 1 - u)
                    dve.wait_ge(rows_made, g + 1)
                    dve.wait_ge(place_made, g + 1)
                    for j in range(G):
                        dve.scalar_tensor_tensor(junk[:, u, j, :], rows[:, u, j, :], c.src[:, bass.ds(g * G + j, 1)],
                                                 c.before[:, :], ALU.is_equal, ALU.mult,
                                                 accum_out=in_tile[:, u, j:j + 1]).then_inc(sums, 1)
                        dve.wait_ge(looked, g * G + j + 1)
                        dve.tensor_tensor_reduce(junk_l[:, u, j, :], look[:, j % 2, 0:NB], hi_hot[:, u, j, :], 1.0, 0.0,
                                                 ALU.mult, ALU.add, before[:, u, j:j + 1]).then_inc(sums, 1)
                    dve.wait_ge(sums, (g + 1) * 2 * G + 4)
                    dve.wait_ge(scattered[u], i * (16 * G) + 16)
                    dve.tensor_tensor(place[:, u, :], in_tile[:, u, :], before[:, u, :], ALU.add)\
                        .then_inc(place_made, 1)

        @block.tensor
        def _(pe):
            def turn(g, u):
                pe.wait_ge(hots_made, g * 2 + 2)
                if not (isinstance(g, int) and g == 0):
                    pe.wait_ge(lo_ready, g * 4)
                for j in range(G):
                    last = pe.transpose(lo_ps[:, j, :], lo_hot[:, u, j, :], c.ident_bf[:, :])
                last.then_inc(turned, 1)
                pe.wait_ge(cols_made, g + 1)
                for j in range(G):
                    last = pe.matmul(rows[:, u, j, :], bc(cols[:, u, j:j + 1], [P, P]), c.ident[:, :],
                                     start=True, stop=True)
                last.then_inc(rows_made, 1)

            pe.matmul(run[:, 0:NB], c.ident[:, :], c.base[:, 0, :], start=True, stop=True).then_inc(updated, 1)
            turn(0, 0)
            with pe.Fori(0, NG // 2) as i:
                for u in range(2):
                    g = i * 2 + u
                    for j in range(G):
                        pe.wait_ge(lo_ready, g * 4 + j // 2 + 1)
                        pe.wait_ge(table_ready, g * G + j + 1)
                        pe.wait_ge(sums, g * 2 * G + 2 * j + 2)
                        pe.matmul(look[:, j % 2, 0:NB], lo_t[:, u, j, :], table[:, j % 2, :],
                                  start=True, stop=True).then_inc(looked, 1)
                        pe.matmul(run[:, 0:NB], lo_hot[:, u, j, :], hi_hot[:, u, j, :],
                                  start=False, stop=True, skip_group_check=True).then_inc(updated, 1)
                        if j == 3:
                            turn(g + 1, 1 - u)

        @block.scalar
        def _(act):
            def take_cols(g, u):
                act.activation(cols[:, u, :], c.src[:, bass.ds(g * G, G)], ACT.Copy).then_inc(cols_made, 1)

            def take_lo(u, q):
                act.activation(lo_t[:, u, 2 * q:2 * q + 2, :], lo_ps[:, 2 * q:2 * q + 2, :], ACT.Copy)\
                    .then_inc(lo_ready, 1)

            take_cols(0, 0)
            act.wait_ge(updated, 1)
            act.activation(table[:, 0, :], run[:, 0:NB], ACT.Copy).then_inc(table_ready, 1)
            act.wait_ge(turned, 1)
            for q in range(4):
                take_lo(0, q)
            with act.Fori(0, NG // 2) as i:
                for u in range(2):
                    g = i * 2 + u
                    act.wait_ge(rows_made, g + 1)
                    take_cols(g + 1, 1 - u)
                    act.wait_ge(scattered[u], i * (16 * G) + 16)
                    act.activation(rec[:, u, :, :], c.rec[:, bass.ds(g * G, G), :], ACT.Copy).then_inc(rec_ready, 1)
                    for j in range(G):
                        act.wait_ge(updated, g * G + j + 2)
                        act.activation(table[:, (j + 1) % 2, :], run[:, 0:NB], ACT.Copy).then_inc(table_ready, 1)
                        if j == 4:
                            act.wait_ge(turned, g + 2)
                        if j >= 4:
                            take_lo(1 - u, j - 4)

        @block.gpsimd
        def _(pool):
            pool.wait_ge(tail_made, 1)
            for u in range(2):
                pool.dma_start(d.rec[EP + u * P:EP + (u + 1) * P, :], tail[:, u, :]).then_inc(scattered[u], 16)
            with pool.Fori(0, NG // 2) as i:
                for u in range(2):
                    g = i * 2 + u
                    pool.wait_ge(place_made, g + 3)
                    pool.wait_ge(rec_ready, g + 1)
                    pool.sem_inc(pool_turn, 1)
                    for j in range(G):
                        pool.indirect_dma_start(
                            out=d.rec, out_offset=bass.IndirectOffsetOnAxis(ap=place[:, u, j:j + 1], axis=0),
                            in_=rec[:, u, j, :], in_offset=None).then_inc(scattered[u], 16)
            for u in range(2):
                pool.wait_ge(scattered[u], (NG // 2) * 16 * G + 16)


def gather_rows(nc, c, d, sem, turn, name, table, width, rec, rec_width, index_word, rows):
    loaded = [sem(f"{name}_loaded{u}") for u in range(RING)]
    gathered, base = c.gathered, turn * (NG // RING) * 16 * G
    stored = [sem(f"{name}_stored{u}") for u in range(RING)]
    pool_turn = sem(f"{name}_pool_turn")
    tail_made = sem(f"{name}_tail_made")
    whole = width + rec_width
    rec_v = rec[0:EP, :].rearrange("(p t) w -> p t w", t=NT)
    rows_v = rows[0:EP, :].rearrange("(p t) w -> p t w", t=NT)
    with nc.Block() as block, ExitStack() as ctx:
        sb, _, _ = allocators(nc, ctx)
        ring = sb(f"{name}_ring", [P, RING, G, whole])
        tail = sb(f"{name}_tail", [2 * P // RING, RING, whole])

        @block.vector
        def _(dve):
            dve.memset(tail[:, :, :], -1.0).then_inc(tail_made, 1)

        @block.sync
        def _(sp):
            with sp.Fori(0, NG // RING) as i:
                for u in range(RING):
                    sp.wait_ge(stored[u], i * 16 + 16)
                    sp.dma_start(ring[:, u, :, width:whole], rec_v[:, bass.ds((i * RING + u) * G, G), :])\
                        .then_inc(loaded[u], 16)

        @block.gpsimd
        def _(pool):
            with pool.Fori(0, NG // RING) as i:
                for u in range(RING):
                    pool.wait_ge(loaded[u], i * 16 + 16)
                    pool.sem_inc(pool_turn, 1)
                    for j in range(G):
                        at = ring[:, u, j, width + index_word:width + index_word + 1].bitcast(U32)
                        pool.indirect_dma_start(
                            out=ring[:, u, j, 0:width], out_offset=None, in_=table,
                            in_offset=bass.IndirectOffsetOnAxis(ap=at, axis=0)).then_inc(gathered[u], 16)

        @block.scalar
        def _(act):
            act.wait_ge(tail_made, 1)
            for u in range(RING):
                n = 2 * P // RING
                act.dma_start(rows[EP + u * n:EP + (u + 1) * n, :], tail[:, u, :]).then_inc(stored[u], 16)
            with act.Fori(0, NG // RING) as i:
                for u in range(RING):
                    act.wait_ge(gathered[u], (i + 1) * (16 * G) + base)
                    act.dma_start(rows_v[:, bass.ds((i * RING + u) * G, G), :], ring[:, u, :, :])\
                        .then_inc(stored[u], 16)
            for u in range(RING):
                act.wait_ge(stored[u], NG // RING * 16 + 16)


def window_loop(eng, passes, body, after=None, before=None, end=None):
    n = eng.value_load(passes, min_val=1, max_val=EP // P)
    with eng.Fori(0, n) as o:
        if before is not None:
            before(o)
        with eng.Fori(0, NB) as b:
            for q in range(NQ):
                body(b, o * NB + b, q)
            if after is not None:
                after(b, o * NB + b)
        if end is not None:
            end(o)


class Offsets:

    def __init__(self, sb, sem, name, first):
        self.first = first
        self.now = sb(f"{name}_off_now", [1, NB * NW], I32)
        self.ready, self.taken = (sem(f"{name}_off_{x}") for x in ("ready", "taken"))

    def load(self, sp):
        sp.dma_start(self.now[0:1, :], self.first.rearrange("(a w) -> a w", a=1)).then_inc(self.ready, 16)

    def next_pass(self, sp, o):
        sp.wait_ge(self.ready, o + 16)
        sp.sem_inc(self.taken, 1)

    def step(self, dve, o):
        dve.wait_ge(self.ready, o + 16)
        dve.tensor_scalar(self.now[:, :], self.now[:, :], float(P), float(EP), ALU.add, ALU.min)\
            .then_inc(self.ready, 1)
        dve.wait_ge(self.ready, o + 17)
        dve.sem_inc(self.taken, 1)


def conv(nc, c, d, sem, name, rows, width, feats, outs, weight, conv_out, moved):
    word = width
    loaded = [sem(f"{name}_loaded{u}") for u in range(NQ)]
    outer_made = sem(f"{name}_outer")
    spread_made = sem(f"{name}_spread")
    dve_seq = sem(f"{name}_dve")
    summed = sem(f"{name}_summed")
    taken = sem(f"{name}_taken")
    batch_done = sem(f"{name}_batch_done")
    mixed = sem(f"{name}_mixed")
    mixed_taken = sem(f"{name}_mixed_taken")
    turned = sem(f"{name}_turned")
    added = sem(f"{name}_added")
    weight_loaded = sem(f"{name}_weight")
    cleared = sem(f"{name}_cleared")
    pair = 2 * WN * feats
    part = G // SPREADS
    with nc.Block() as block, ExitStack() as ctx:
        sb, ps, _ = allocators(nc, ctx)
        rin = sb(f"{name}_rin", [P, NQ, G, width + ROW])
        mark = sb(f"{name}_mark", [P, NQ, G, WN])
        basis = sb(f"{name}_basis_sb", [P, NQ, G, 25, 5])
        spread = sb(f"{name}_spread_sb", [P, NQ, G, WN, feats])
        plane = sb(f"{name}_plane", [P, NQ, G, 5, 5])
        hat = sb(f"{name}_hat", [P, NQ, G, 3, 5])
        rel, pos = sb(f"{name}_rel", [P, G]), sb(f"{name}_pos", [P, G, 3])
        up, down = sb(f"{name}_up", [P, G * 3, 5]), sb(f"{name}_down", [P, G * 3, 5])
        sums = sb(f"{name}_sums", [K, P, feats])
        wsb = sb(f"{name}_w", [K, feats, outs])
        mix_sb = sb(f"{name}_mix_sb", [outs, P])
        offsets = Offsets(sb, sem, name, d.off[0])
        acc = [ps(f"{name}_acc{k}", [K, 512]) for k in range(4)]
        mix = ps(f"{name}_mix", [P, 512])
        back = ps(f"{name}_back", [P, 512])
        if moved is not None:
            trow = sb(f"{name}_trow", [P, NQ, G * WN, 4])
            tsel = sb(f"{name}_tsel", [P, G, WN, 3])
            tsrc = sb(f"{name}_tsrc", [P, G, 3])

        @block.sync
        def _(sp):
            offsets.load(sp)
            sp.dma_start(wsb[:, :, :], weight).then_inc(weight_loaded, 16)

            def next_pass(o):
                offsets.next_pass(sp, o)

            def body(b, item, q):
                sp.wait_ge(batch_done, item * NQ + q + 1)
                _, offs = nc.values_load_multi_w_load_instructions(
                    offsets.now[0:1, bass.ds(b * NW + q * G, G)], engines=(sp.engine,), min_val=0, max_val=EP)
                for w in range(G):
                    sp.dma_start(rin[:, q, w, :], rows[bass.ds(offs[w], P), :]).then_inc(loaded[q], 16)
                if moved is not None:
                    sp.dma_start(trow[:, q, :, :].rearrange("p n k -> p (n k)"),
                                 bc(moved[bass.ds(b * P + q * G * WN, G * WN), :].rearrange("n k -> (n k)").unsqueeze(0),
                                    [P, G * WN * 4])).then_inc(loaded[q], 16)
            window_loop(sp, c.passes[0], body, before=next_pass)

        @block.vector
        def _(dve):
            dve.memset(conv_out, 0.0).then_inc(cleared, 1)
            dve.wait_ge(cleared, 1)
            dve.sem_inc(added, 1)
            steps = 9 if moved is None else 13
            loads = 16 * (G if moved is None else G + 1)

            def body(b, item, q):
                m = item * NQ + q

                def after_step(n):
                    dve.wait_ge(dve_seq, m * steps + n)

                def make_spread(k):
                    w = slice(k * part, (k + 1) * part)
                    dve.tensor_tensor(spread[:, q, w, :, :], bc(mark[:, q, w, :].unsqueeze(3), [P, part, WN, feats]),
                                      bc(rin[:, q, w, 0:feats].unsqueeze(2), [P, part, WN, feats]), ALU.mult)\
                        .then_inc(spread_made, 1)

                dve.wait_ge(loaded[q], (item + 1) * loads)
                attr = rin[:, q, :, word + 2:word + 5]
                dve.tensor_scalar(rel[:, :], rin[:, q, :, word], c.first[:, bass.ds(b, 1)], None, ALU.subtract)\
                    .then_inc(dve_seq, 1)
                if moved is None:
                    dve.tensor_copy(pos[:, :, :], attr).then_inc(dve_seq, 1)
                    after_step(1)
                    dve.tensor_tensor(mark[:, q, :, :], bc(rel[:, :].unsqueeze(2), [P, G, WN]),
                                      c.window_ramp[:, q, :, :], ALU.is_equal).then_inc(dve_seq, 1)
                    after_step(2)
                    first = 3
                else:
                    dve.tensor_tensor(pos[:, :, :], attr, rin[:, q, :, feats:feats + 3], ALU.add).then_inc(dve_seq, 1)
                    after_step(1)
                    dve.tensor_tensor(mark[:, q, :, :], bc(rel[:, :].unsqueeze(2), [P, G, WN]),
                                      c.window_ramp[:, q, :, :], ALU.is_equal).then_inc(dve_seq, 1)
                    after_step(3)
                    dve.tensor_tensor(tsel[:, :, :, :].rearrange("p g r k -> p (g r) k"),
                                      bc(mark[:, q, :, :].rearrange("p g r -> p (g r)").unsqueeze(2),
                                         [P, G * WN, 3]), trow[:, q, :, 0:3], ALU.mult).then_inc(dve_seq, 1)
                    make_spread(0)
                    after_step(4)
                    dve.tensor_reduce(tsrc[:, :, :], tsel[:, :, :, :].rearrange("p g r k -> p g k r"), X, ALU.add)\
                        .then_inc(dve_seq, 1)
                    make_spread(1)
                    after_step(5)
                    dve.tensor_tensor(pos[:, :, :], pos[:, :, :], tsrc[:, :, :], ALU.subtract).then_inc(dve_seq, 1)
                    make_spread(2)
                    after_step(6)
                    dve.tensor_scalar(pos[:, :, :], pos[:, :, :], 0.0, 1.0, ALU.max, ALU.min).then_inc(dve_seq, 1)
                    make_spread(3)
                    after_step(7)
                    first = 7
                flat = bc(pos[:, :, :].rearrange("p g k -> p (g k)").unsqueeze(2), [P, G * 3, 5])
                for side, scale, knots, op in ((up, 4.0, c.jm, ALU.subtract), (down, -4.0, c.jp, ALU.add)):
                    dve.scalar_tensor_tensor(side[:, :, :], flat, scale, bc(knots[:, :].unsqueeze(1), [P, G * 3, 5]),
                                             ALU.mult, op).then_inc(dve_seq, 1)
                after_step(first + 1)
                dve.tensor_tensor(up[:, :, :], up[:, :, :], bc(c.up_floor[:, :].unsqueeze(1), [P, G * 3, 5]),
                                  ALU.max).then_inc(dve_seq, 1)
                after_step(first + 2)
                dve.tensor_tensor(down[:, :, :], down[:, :, :], bc(c.down_floor[:, :].unsqueeze(1), [P, G * 3, 5]),
                                  ALU.max).then_inc(dve_seq, 1)
                if moved is None and feats > 1:
                    for k in range(SPREADS // 2):
                        make_spread(k)
                after_step(first + 4)
                dve.tensor_tensor(hat[:, q, :, :, :].rearrange("p g k j -> p (g k) j"), up[:, :, :],
                                  down[:, :, :], ALU.min).then_inc(dve_seq, 1)
                if moved is None and feats > 1:
                    for k in range(SPREADS // 2, SPREADS):
                        make_spread(k)
                after_step(steps - 1)
                dve.tensor_tensor(plane[:, q, :, :, :], bc(hat[:, q, :, 0, :].unsqueeze(3), [P, G, 5, 5]),
                                  bc(hat[:, q, :, 1, :].unsqueeze(2), [P, G, 5, 5]), ALU.mult).then_inc(dve_seq, 1)
                if q == NQ - 1:
                    dve.wait_ge(dve_seq, (m + 1) * steps)

            def step(o):
                offsets.step(dve, o)

            window_loop(dve, c.passes[0], body, end=step)

        @block.gpsimd
        def _(pool):
            steps = 9 if moved is None else 13

            def body(b, item, q):
                pool.wait_ge(dve_seq, (item * NQ + q + 1) * steps)
                pool.tensor_tensor(
                    basis[:, q, :, :, :],
                    bc(plane[:, q, :, :, :].rearrange("p g a b -> p g (a b)").unsqueeze(3), [P, G, 25, 5]),
                    bc(hat[:, q, :, 2, :].unsqueeze(2), [P, G, 25, 5]), ALU.mult).then_inc(outer_made, 1)
            window_loop(pool, c.passes[0], body)

        @block.tensor
        def _(pe):
            pe.wait_ge(weight_loaded, 16)
            pe.matmul(mix[0:1, 0:1], c.zeros[:, 0:1], c.zeros[:, 0:1], start=True, stop=True).then_inc(batch_done, NQ)

            def body(b, item, q):
                pe.wait_ge(outer_made, item * NQ + q + 1)
                if feats > 1:
                    pe.wait_ge(spread_made, (item * NQ + q + 1) * SPREADS)
                for w in range(G):
                    pp = q * (G // 2) + w // 2
                    if w % 2 == 0:
                        pe.wait_ge(taken, item * (NW // 2) + pp + 1)
                    rhs = spread[:, q, w, :, :].rearrange("p n f -> p (n f)") if feats > 1 else mark[:, q, w, :]
                    last = pe.matmul(acc[pp % 4][:, (w % 2) * WN * feats:(w % 2 + 1) * WN * feats],
                                     basis[:, q, w, :, :].rearrange("p a b -> p (a b)"), rhs, start=True, stop=True)
                    if w % 2:
                        last.then_inc(summed, 1)
                pe.wait_ge(summed, item * (NW // 2) + (q + 1) * (G // 2))
                pe.sem_inc(batch_done, 1)

            def after(b, item):
                pe.wait_ge(taken, (item + 1) * (NW // 2) + 4)
                for f in range(feats):
                    last = pe.matmul(mix[0:outs, 0:P], wsb[:, f, :], sums[:, :, f], start=(f == 0), stop=(f == feats - 1))
                last.then_inc(mixed, 1)
                pe.wait_ge(added, item + 1)
                pe.matmul(back[:, 0:outs], c.ident[:, :],
                          conv_out[:, bass.ds(b, 1), :].rearrange("p b o -> p (b o)"), start=True, stop=False)
                pe.wait_ge(mixed_taken, item + 1)
                pe.matmul(back[:, 0:outs], mix_sb[:, :], c.ident[0:outs, 0:outs], start=False, stop=True)\
                    .then_inc(turned, 1)
            window_loop(pe, c.passes[0], body, after)

        @block.scalar
        def _(act):
            act.sem_inc(taken, 4)

            def body(b, item, q):
                for h in range(G // 2):
                    pp = q * (G // 2) + h
                    act.wait_ge(summed, item * (NW // 2) + pp + 1)
                    act.activation(sums[:, pp * 2 * WN:(pp + 1) * 2 * WN, :].rearrange("p n f -> p (n f)"),
                                   acc[pp % 4][:, 0:pair], ACT.Copy).then_inc(taken, 1)

            def after(b, item):
                act.wait_ge(mixed, item + 1)
                act.activation(mix_sb[:, :], mix[0:outs, 0:P], ACT.Copy).then_inc(mixed_taken, 1)
                act.wait_ge(turned, item + 1)
                act.activation(conv_out[:, bass.ds(b, 1), :].rearrange("p b o -> p (b o)"), back[:, 0:outs], ACT.Copy)\
                    .then_inc(added, 1)
            window_loop(act, c.passes[0], body, after)


def broadcast_row(row, n):
    return bc(row.rearrange("(a n) -> a n", a=1), [P, n])


def elu(dve, chain, act_turn, act_done, turn, v, low):
    chain(dve.tensor_scalar(low, v, 0.0, None, ALU.min))
    dve.sem_inc(act_turn, 1)
    dve.wait_ge(act_done, turn)
    chain(dve.scalar_tensor_tensor(v, v, 0.0, low, ALU.max, ALU.add))
    chain(dve.tensor_scalar(v, v, -1.0, None, ALU.add))


def conv_to_hidden(nc, c, d, sem, name, hid, bias_dram, table):
    loaded, chain_sem = sem(f"{name}_loaded"), sem(f"{name}_chain")
    low_ready, exp_ready, stored, made = (sem(f"{name}_{x}") for x in ("low", "exp", "stored", "made"))
    with nc.Block() as block, ExitStack() as ctx:
        sb, _, _ = allocators(nc, ctx)
        low = sb(f"{name}_low_sb", [P, NB, HID])
        bias = sb(f"{name}_bias", [P, HID])

        @block.sync
        def _(sp):
            sp.dma_start(bias[:, :], broadcast_row(bias_dram, HID)).then_inc(loaded, 16)
            if table is not None:
                sp.wait_ge(made, 1)
                sp.dma_start(node_view(table, HID), hid).then_inc(stored, 16)
                sp.wait_ge(stored, 16)

        @block.scalar
        def _(act):
            act.wait_ge(low_ready, 1)
            act.activation(low[:, :, :], low[:, :, :], ACT.Exp).then_inc(exp_ready, 1)

        @block.vector
        def _(dve):
            chain = Chain(dve, chain_sem)
            chain(dve.tensor_scalar(c.rdeg[:, :], c.deg[:, :], 1.0, None, ALU.max))
            chain(dve.reciprocal(c.rdeg[:, :], c.rdeg[:, :]))
            chain(dve.tensor_tensor(hid, hid, bc(c.rdeg[:, :].unsqueeze(2), [P, NB, HID]), ALU.mult))
            dve.wait_ge(loaded, 16)
            chain(dve.tensor_tensor(hid, hid, bc(bias[:, :].unsqueeze(1), [P, NB, HID]), ALU.add))
            elu(dve, chain, low_ready, exp_ready, 1, hid, low[:, :, :])
            dve.sem_inc(made, 1)


RING = 4
SET = 7


def move_table(nc, c, d, sem, hid):
    loaded, chain_sem = sem("mt_loaded"), sem("mt_chain")
    turned, copied, mixed, biased, low_ready, exp_ready, hidden, moved, moved_taken, made, stored = (
        sem(f"mt_{x}") for x in ("turned", "copied", "mixed", "biased", "low", "exp", "hidden", "moved",
                                 "moved_taken", "made", "stored"))
    cols = SET * P
    halves = ((0, 512), (512, cols))
    with nc.Block() as block, ExitStack() as ctx:
        sb, ps, _ = allocators(nc, ctx)
        w3, b3, w4, b4 = sb("w3", [HID, HID]), sb("b3", [HID, 1]), sb("w4", [HID, 3]), sb("b4", [P, 3])
        turned_sb, v, low = sb("mt_t", [HID, cols]), sb("mt_v", [HID, cols]), sb("mt_l", [HID, cols])
        t_all = sb("mt_all", [P, NB, 4])
        table = sb("mt_table", [P, NB, 36])
        turned_ps, mix_ps, t_ps = ps("mt_tp", [HID, 1024]), ps("mt_mp", [HID, 1024]), ps("mt_op", [P, 512])

        @block.sync
        def _(sp):
            sp.dma_start(w3[:, :], d.stn3_w).then_inc(loaded, 16)
            sp.dma_start(b3[:, :], d.stn3_b.rearrange("(o a) -> o a", a=1)).then_inc(loaded, 16)
            sp.dma_start(w4[:, :], d.stn4_w).then_inc(loaded, 16)
            sp.dma_start(b4[:, :], broadcast_row(d.stn4_b, 3)).then_inc(loaded, 16)
            sp.wait_ge(made, 1)
            sp.dma_start(node_view(d.move, 4), t_all[:, :, :]).then_inc(stored, 16)
            sp.dma_start(node_view(d.feat_table, 36), table[:, :, :]).then_inc(stored, 16)
            sp.wait_ge(stored, 32)

        @block.tensor
        def _(pe):
            pe.wait_ge(loaded, 64)
            for s in range(NB // SET):
                if s:
                    pe.wait_ge(copied, s)
                for j in range(SET):
                    last = pe.transpose(turned_ps[:, j * P:(j + 1) * P], hid[:, s * SET + j, :], c.ident[:, :])
                last.then_inc(turned, 1)
                pe.wait_ge(copied, s + 1)
                if s:
                    pe.wait_ge(biased, s)
                for a, z in halves:
                    last = pe.matmul(mix_ps[:, a:z], w3[:, :], turned_sb[:, a:z], start=True, stop=True)
                last.then_inc(mixed, 1)
                pe.wait_ge(hidden, s + 1)
                if s:
                    pe.wait_ge(moved_taken, s)
                for j in range(SET):
                    last = pe.matmul(t_ps[:, 4 * j:4 * j + 3], v[:, j * P:(j + 1) * P], w4[:, :], start=True, stop=True)
                last.then_inc(moved, 1)

        @block.scalar
        def _(act):
            act.wait_ge(loaded, 64)
            for s in range(NB // SET):
                act.wait_ge(turned, s + 1)
                act.activation(turned_sb[:, :], turned_ps[:, 0:cols], ACT.Copy).then_inc(copied, 1)
                act.wait_ge(mixed, s + 1)
                if s:
                    act.wait_ge(moved, s)
                act.activation(v[:, :], mix_ps[:, 0:cols], ACT.Identity, bias=b3[:, 0:1]).then_inc(biased, 1)
                act.wait_ge(low_ready, s + 1)
                act.activation(low[:, :], low[:, :], ACT.Exp).then_inc(exp_ready, 1)

        @block.vector
        def _(dve):
            chain = Chain(dve, chain_sem)
            chain(dve.memset(t_all[:, :, :], 0.0))
            chain(dve.memset(table[:, :, :], 0.0))
            chain(dve.tensor_copy(table[:, :, 0:FEAT], c.h[:, :, :]))
            dve.wait_ge(loaded, 64)
            for s in range(NB // SET):
                dve.wait_ge(biased, s + 1)
                elu(dve, chain, low_ready, exp_ready, s + 1, v[:, :], low[:, :])
                dve.sem_inc(hidden, 1)
                dve.wait_ge(moved, s + 1)
                chain(dve.tensor_tensor(t_all[:, s * SET:(s + 1) * SET, 0:3],
                                        t_ps[:, 0:4 * SET].rearrange("p (j k) -> p j k", k=4)[:, :, 0:3],
                                        bc(b4[:, :].unsqueeze(1), [P, SET, 3]), ALU.add))
                dve.sem_inc(moved_taken, 1)
            chain(dve.tensor_copy(table[:, :, FEAT:FEAT + 3], t_all[:, :, 0:3]))
            dve.sem_inc(made, 1)


def second_norm(nc, c, d, sem):
    loaded, chain_sem, cleared = sem("n2_loaded"), sem("n2_chain"), sem("n2_cleared")
    var_ready, std_ready, weights_ready, normed, turned, copied, scored, scored_taken = (
        sem(f"n2_{x}") for x in ("var", "std", "weights", "normed", "turned", "copied", "scored", "scored_taken"))
    low_made, low_turned, low_done, low_spread, made, stored = (
        sem(f"n2_{x}") for x in ("low", "low_turned", "low_done", "low_spread", "made", "stored"))
    cols = SET * P
    with nc.Block() as block, ExitStack() as ctx:
        sb, ps, _ = allocators(nc, ctx)
        bias = sb("n2_bias", [P, FEAT])
        wg = sb("n2_wg", [FEAT, HEADS * FEAT])
        attn = sb("n2_attn", [FEAT, 2, HEADS * FEAT])
        prod = sb("n2_prod", [FEAT, 2, HEADS * FEAT])
        score_w = sb("n2_score_w", [FEAT, 2 * HEADS])
        tmp, stat = sb("n2_tmp", [P, NB, FEAT]), sb("n2_stat", [P, 3, NB])
        h_t = sb("n2_ht", [FEAT, cols])
        table = sb("n2_table", [P, NB, 40])
        low, low_row = sb("n2_low", [P, 1]), sb("n2_low_row", [1, 1])
        turned_ps, score_ps, low_ps = ps("n2_tp", [FEAT, 1024]), ps("n2_sp", [P, 512]), ps("n2_lp", [P, 512])

        @block.sync
        def _(sp):
            sp.dma_start(bias[:, :], broadcast_row(d.conv_b, FEAT)).then_inc(loaded, 16)
            sp.dma_start(wg[:, :], d.W_gat).then_inc(loaded, 16)
            for k, a in enumerate((d.attn_l, d.attn_r)):
                sp.dma_start(attn[:, k, :], bc(a.rearrange("(a h) f -> a (h f)", a=1), [FEAT, HEADS * FEAT]))\
                    .then_inc(loaded, 16)
            sp.wait_ge(made, 1)
            sp.dma_start(node_view(d.gat_table, 40), table[:, :, :]).then_inc(stored, 16)
            sp.wait_ge(stored, 16)

        @block.scalar
        def _(act):
            act.wait_ge(var_ready, 1)
            act.activation(stat[:, 2, :], stat[:, 1, :], ACT.Sqrt).then_inc(std_ready, 1)
            for s in range(NB // SET):
                act.wait_ge(turned, s + 1)
                if s:
                    act.wait_ge(scored, s)
                act.activation(h_t[:, :], turned_ps[:, 0:cols], ACT.Copy).then_inc(copied, 1)

        @block.tensor
        def _(pe):
            pe.wait_ge(normed, 1)
            for s in range(NB // SET):
                if s:
                    pe.wait_ge(copied, s)
                for j in range(SET):
                    last = pe.transpose(turned_ps[:, j * P:(j + 1) * P], c.h[:, s * SET + j, :], c.ident[:, :])
                last.then_inc(turned, 1)
                pe.wait_ge(copied, s + 1)
                if s:
                    pe.wait_ge(scored_taken, s)
                for j in range(SET):
                    last = pe.matmul(score_ps[:, 8 * j:8 * j + 8], h_t[:, j * P:(j + 1) * P], score_w[:, :],
                                     start=True, stop=True)
                last.then_inc(scored, 1)
            pe.wait_ge(low_made, 1)
            pe.transpose(low_ps[0:1, 0:P], low[:, :], c.ident[:, :]).then_inc(low_turned, 1)
            pe.wait_ge(low_done, 1)
            pe.matmul(low_ps[:, 0:1], c.ones[0:1, :], low_row[:, :], start=True, stop=True).then_inc(low_spread, 1)

        @block.vector
        def _(dve):
            chain = Chain(dve, chain_sem)
            dve.wait_ge(loaded, 64)
            chain(dve.tensor_tensor(c.sum3[:, :, :], c.sum3[:, :, :], bc(c.rdeg[:, :].unsqueeze(2), [P, NB, FEAT]),
                                    ALU.mult))
            chain(dve.tensor_tensor(c.sum3[:, :, :], c.sum3[:, :, :], bc(bias[:, :].unsqueeze(1), [P, NB, FEAT]),
                                    ALU.add))
            chain(dve.tensor_tensor(c.x[:, :, :], c.x[:, :, :], c.sum3[:, :, :], ALU.add))
            layer_norm_relu(dve, chain, var_ready, std_ready, 1, c.h[:, :, :], c.x[:, :, :], tmp[:, :, :], stat)
            for k in range(2):
                chain(dve.tensor_tensor(prod[:, k, :], wg[:, :], attn[:, k, :], ALU.mult))
            chain(dve.tensor_reduce(score_w[:, :], prod[:, :, :].rearrange("p k (h f) -> p (k h) f", f=FEAT), X,
                                    ALU.add))
            dve.sem_inc(normed, 1)
            chain(dve.memset(table[:, :, :], 0.0))
            chain(dve.memset(table[:, :, FEAT:FEAT + 1], 1.0))
            chain(dve.tensor_copy(table[:, :, 0:FEAT], c.h[:, :, :]))
            for s in range(NB // SET):
                dve.wait_ge(scored, s + 1)
                chain(dve.tensor_copy(c.elr[:, s * SET:(s + 1) * SET, :],
                                      score_ps[:, 0:8 * SET].rearrange("p (j k) -> p j k", k=8)))
                dve.sem_inc(scored_taken, 1)
            chain(dve.tensor_copy(table[:, :, FEAT + 1:FEAT + 5], c.elr[:, :, 0:HEADS]))
            dve.sem_inc(made, 1)
            chain(dve.tensor_reduce(low[:, :], c.elr[:, :, 0:HEADS], mybir.AxisListType.XY, ALU.min))
            dve.sem_inc(low_made, 1)
            dve.wait_ge(low_turned, 1)
            chain(dve.tensor_reduce(low_row[:, :], low_ps[0:1, 0:P], X, ALU.min))
            dve.sem_inc(low_done, 1)
            dve.wait_ge(low_spread, 1)
            chain(dve.tensor_scalar(c.shift[:, :], low_ps[:, 0:1], -1.0, 1.0, ALU.mult, ALU.add))


GW = 42


def attention_max(nc, c, d, sem):
    loaded = [sem(f"mx_loaded{u}") for u in range(2)]
    in_free, dve_seq, spread_made, turned, chain_sem = (
        sem(f"mx_{x}") for x in ("in_free", "dve", "spread", "turned", "chain"))
    max_made, out_turned, out_copied, stored, read, made, er_stored = (
        sem(f"mx_{x}") for x in ("max_made", "out_turned", "out_copied", "stored", "read", "made", "er_stored"))
    steps = 7
    with nc.Block() as block, ExitStack() as ctx:
        sb, ps, _ = allocators(nc, ctx)
        rin = sb("mx_rin", [P, 2, G, GW - FEAT])
        rel, mark = sb("mx_rel", [P, 2, G]), sb("mx_mark", [P, 2, G, WN])
        el = sb("mx_el", [P, 2, G, HEADS])
        spread = sb("mx_spread_sb", [P, 2, G, WN, HEADS])
        top = sb("mx_top", [P, 2])
        best = sb("mx_best", [P, NB * NQ])
        best_t = sb("mx_best_t", [NB, NQ, P])
        best_node = sb("mx_node", [P, NB, HEADS])
        er_max = sb("mx_er_max", [P, NB, 2 * HEADS])
        turned_ps = ps("mx_tp", [P, 2, 512])
        offsets = Offsets(sb, sem, "mx", d.off[1])
        out_ps = ps("mx_op", [NB, 512])

        @block.sync
        def _(sp):
            offsets.load(sp)

            def next_pass(o):
                offsets.next_pass(sp, o)

            def body(b, item, q):
                u = q % 2
                sp.wait_ge(in_free, item * NQ + q + 1)
                _, offs = nc.values_load_multi_w_load_instructions(
                    offsets.now[0:1, bass.ds(b * NW + q * G, G)], engines=(sp.engine,), min_val=0, max_val=EP)
                for w in range(G):
                    sp.dma_start(rin[:, u, w, :], d.rows4[bass.ds(offs[w], P), FEAT:GW]).then_inc(loaded[u], 16)
            window_loop(sp, c.passes[1], body, before=next_pass)
            sp.wait_ge(out_copied, 1)
            sp.dma_start(d.best.rearrange("(b q x) -> b q x", q=NQ, x=P), best_t[:, :, :]).then_inc(stored, 16)
            sp.wait_ge(stored, 16)
            sp.dma_start(best_node[:, :, :], d.best.rearrange("(b p h) -> p b h", p=P, h=HEADS)).then_inc(read, 16)
            sp.wait_ge(made, 1)
            sp.dma_start(node_view(d.er_max, 2 * HEADS), er_max[:, :, :]).then_inc(er_stored, 16)
            sp.wait_ge(er_stored, 16)

        @block.vector
        def _(dve):
            chain = Chain(dve, chain_sem)
            chain(dve.memset(best[:, :], 0.0))
            dve.sem_inc(in_free, 2)

            def body(b, item, q):
                u = q % 2
                m = item * NQ + q
                n = [0]

                def own(ins):
                    n[0] += 1
                    ins.then_inc(dve_seq, 1)
                    dve.wait_ge(dve_seq, m * steps + n[0])

                dve.wait_ge(loaded[u], (item * 2 + q // 2 + 1) * (16 * G))
                dve.wait_ge(turned, m + 1)
                own(dve.tensor_scalar(rel[:, u, :], rin[:, u, :, GW - FEAT - 1], c.first[:, bass.ds(b, 1)], None,
                                      ALU.subtract))
                own(dve.tensor_scalar(el[:, u, :, :], rin[:, u, :, 1:1 + HEADS], c.shift[:, 0:1], None, ALU.add))
                own(dve.tensor_tensor(mark[:, u, :, :], bc(rel[:, u, :].unsqueeze(2), [P, G, WN]),
                                      c.window_ramp[:, q, :, :], ALU.is_equal))
                dve.sem_inc(in_free, 1)
                own(dve.tensor_tensor(spread[:, u, :, :, :], bc(mark[:, u, :, :].unsqueeze(3), [P, G, WN, HEADS]),
                                      bc(el[:, u, :, :].unsqueeze(2), [P, G, WN, HEADS]), ALU.mult))
                dve.sem_inc(spread_made, 1)
                dve.wait_ge(turned, m + 3)
                own(dve.tensor_reduce(top[:, u:u + 1], turned_ps[:, u, 0:P], X, ALU.max))
                at = bass.ds(b * NQ + q, 1)
                own(dve.tensor_tensor(best[:, at], best[:, at], top[:, u:u + 1], ALU.max))
                own(dve.tensor_copy(top[:, u:u + 1], top[:, u:u + 1]))

            def step(o):
                offsets.step(dve, o)

            window_loop(dve, c.passes[1], body, end=step)
            dve.sem_inc(max_made, 1)
            dve.wait_ge(out_turned, 1)
            chain(dve.tensor_copy(best_t[:, :, :], out_ps[:, :].rearrange("b (q x) -> b q x", q=NQ)))
            dve.sem_inc(out_copied, 1)
            dve.wait_ge(read, 16)
            chain(dve.tensor_scalar(best_node[:, :, :], best_node[:, :, :], c.shift[:, 0:1], None, ALU.subtract))
            chain(dve.tensor_copy(er_max[:, :, 0:HEADS], c.elr[:, :, HEADS:2 * HEADS]))
            chain(dve.tensor_tensor(best_node[:, :, :], best_node[:, :, :], er_max[:, :, 0:HEADS], ALU.add))
            chain(dve.scalar_tensor_tensor(er_max[:, :, HEADS:2 * HEADS], best_node[:, :, :], SLOPE,
                                           best_node[:, :, :], ALU.mult, ALU.max))
            dve.sem_inc(made, 1)

        @block.tensor
        def _(pe):
            pe.sem_inc(turned, 2)

            def body(b, item, q):
                u = q % 2
                pe.wait_ge(spread_made, item * NQ + q + 1)
                pe.transpose(turned_ps[:, u, 0:P], spread[:, u, :, :, :].rearrange("p g r h -> p (g r h)"),
                             c.ident[:, :]).then_inc(turned, 1)
            window_loop(pe, c.passes[1], body)
            pe.wait_ge(max_made, 1)
            for q in range(NQ):
                last = pe.transpose(out_ps[:, q * P:(q + 1) * P],
                                    best[:, :].rearrange("p (b q) -> p q b", q=NQ)[:, q, :], c.ident[:, :])
            last.then_inc(out_turned, 1)


def attention_sum(nc, c, d, sem):
    loaded = [sem(f"at_loaded{u}") for u in range(2)]
    in_free, dve_seq, low_ready, exp_ready, weight_made, summed, taken, mixed, added = (
        sem(f"at_{x}") for x in ("in_free", "dve", "low", "exp", "weight", "summed", "taken", "mixed", "added"))
    w_loaded, w_cleared, cleared = sem("at_w_loaded"), sem("at_w_cleared"), sem("at_cleared")
    steps = 9
    F1 = FEAT + 1
    with nc.Block() as block, ExitStack() as ctx:
        sb, ps, _ = allocators(nc, ctx)
        rin = sb("at_rin", [P, 2, G, GW])
        row = sb("at_row", [P, 2, G * WN, 2 * HEADS])
        rel, mark = sb("at_rel", [P, 2, G]), sb("at_mark", [P, 2, G, WN])
        sel = sb("at_sel", [P, 2, G, WN, 2 * HEADS])
        own_er = sb("at_own", [P, 2, G, 2 * HEADS])
        e = sb("at_e", [P, 2, G, HEADS])
        w_exp = sb("at_w", [P, 2, G, HEADS])
        weight = sb("at_weight_sb", [P, 2, G, WN, HEADS])
        agg = sb("at_agg", [F1, P, HEADS])
        wg = sb("at_wg", [F1, HEADS, F1])
        agg_ps = ps("at_agg_ps", [F1, 2, 512])
        offsets = Offsets(sb, sem, "at", d.off[1])
        mix_ps = ps("at_mix_ps", [P, 512])

        @block.sync
        def _(sp):
            offsets.load(sp)
            sp.wait_ge(w_cleared, 1)
            sp.dma_start(wg[0:FEAT, :, 0:FEAT], d.W_gat.rearrange("i (h f) -> i h f", f=FEAT)).then_inc(w_loaded, 16)

            def next_pass(o):
                offsets.next_pass(sp, o)

            def body(b, item, q):
                u = q % 2
                sp.wait_ge(in_free, item * NQ + q + 1)
                _, offs = nc.values_load_multi_w_load_instructions(
                    offsets.now[0:1, bass.ds(b * NW + q * G, G)], engines=(sp.engine,), min_val=0, max_val=EP)
                for w in range(G):
                    sp.dma_start(rin[:, u, w, :], d.rows4[bass.ds(offs[w], P), :]).then_inc(loaded[u], 16)
                sp.dma_start(row[:, u, :, :].rearrange("p n k -> p (n k)"),
                             bc(d.er_max[bass.ds(b * P + q * G * WN, G * WN), :].rearrange("n k -> (n k)").unsqueeze(0),
                                [P, G * WN * 2 * HEADS])).then_inc(loaded[u], 16)
            window_loop(sp, c.passes[1], body, before=next_pass)

        @block.vector
        def _(dve):
            dve.memset(wg[:, :, :], 0.0).then_inc(cleared, 1)
            dve.memset(c.acc[:, :, :], 0.0).then_inc(cleared, 1)
            dve.wait_ge(cleared, 2)
            dve.memset(wg[FEAT:F1, :, FEAT:F1], 1.0).then_inc(w_cleared, 1)
            dve.sem_inc(in_free, 2)
            dve.sem_inc(added, 1)

            def body(b, item, q):
                u = q % 2
                m = item * NQ + q
                n = [0]

                def own(ins):
                    n[0] += 1
                    ins.then_inc(dve_seq, 1)
                    dve.wait_ge(dve_seq, m * steps + n[0])

                dve.wait_ge(loaded[u], (item * 2 + q // 2 + 1) * (16 * (G + 1)))
                dve.wait_ge(summed, m + 1)
                own(dve.tensor_scalar(rel[:, u, :], rin[:, u, :, GW - 1], c.first[:, bass.ds(b, 1)], None,
                                      ALU.subtract))
                own(dve.tensor_tensor(mark[:, u, :, :], bc(rel[:, u, :].unsqueeze(2), [P, G, WN]),
                                      c.window_ramp[:, q, :, :], ALU.is_equal))
                own(dve.tensor_tensor(sel[:, u, :, :, :].rearrange("p g r k -> p (g r) k"),
                                      bc(mark[:, u, :, :].rearrange("p g r -> p (g r)").unsqueeze(2),
                                         [P, G * WN, 2 * HEADS]), row[:, u, :, :], ALU.mult))
                own(dve.tensor_reduce(own_er[:, u, :, :], sel[:, u, :, :, :].rearrange("p g r k -> p g k r"), X,
                                      ALU.add))
                own(dve.tensor_tensor(e[:, u, :, :], rin[:, u, :, F1:F1 + HEADS], own_er[:, u, :, 0:HEADS], ALU.add))
                own(dve.scalar_tensor_tensor(e[:, u, :, :], e[:, u, :, :], SLOPE, e[:, u, :, :], ALU.mult, ALU.max))
                own(dve.tensor_tensor(e[:, u, :, :], e[:, u, :, :], own_er[:, u, :, HEADS:2 * HEADS], ALU.subtract))
                own(dve.tensor_scalar(e[:, u, :, :], e[:, u, :, :], 0.0, None, ALU.min))
                dve.sem_inc(low_ready, 1)
                dve.wait_ge(exp_ready, m + 1)
                own(dve.tensor_tensor(weight[:, u, :, :, :], bc(mark[:, u, :, :].unsqueeze(3), [P, G, WN, HEADS]),
                                      bc(w_exp[:, u, :, :].unsqueeze(2), [P, G, WN, HEADS]), ALU.mult))
                dve.sem_inc(weight_made, 1)

            def after(b, item):
                dve.wait_ge(mixed, item + 1)
                dve.tensor_tensor(c.acc[:, bass.ds(b, 1), :], c.acc[:, bass.ds(b, 1), :],
                                  mix_ps[:, 0:HEADS * F1].unsqueeze(1), ALU.add).then_inc(added, 1)
                dve.wait_ge(added, item + 2)

            def step(o):
                offsets.step(dve, o)

            window_loop(dve, c.passes[1], body, after, end=step)

        @block.scalar
        def _(act):
            act.sem_inc(taken, 2)

            def body(b, item, q):
                u = q % 2
                act.wait_ge(low_ready, item * NQ + q + 1)
                act.activation(w_exp[:, u, :, :], e[:, u, :, :], ACT.Exp).then_inc(exp_ready, 1)
                act.wait_ge(summed, item * NQ + q + 3)
                act.activation(agg[:, q * G * WN:(q + 1) * G * WN, :].rearrange("p n h -> p (n h)"),
                               agg_ps[:, u, 0:P], ACT.Copy).then_inc(taken, 1)
            window_loop(act, c.passes[1], body)

        @block.tensor
        def _(pe):
            pe.sem_inc(summed, 2)
            pe.wait_ge(w_loaded, 16)

            def body(b, item, q):
                u = q % 2
                pe.wait_ge(weight_made, item * NQ + q + 1)
                pe.wait_ge(taken, item * NQ + q + 1)
                for w in range(G):
                    last = pe.matmul(agg_ps[:, u, w * WN * HEADS:(w + 1) * WN * HEADS], rin[:, u, w, 0:F1],
                                     weight[:, u, w, :, :].rearrange("p r h -> p (r h)"), start=True, stop=True)
                last.then_inc(summed, 1)
                pe.wait_ge(summed, item * NQ + q + 3)
                pe.sem_inc(in_free, 1)

            def after(b, item):
                pe.wait_ge(taken, (item + 1) * NQ + 2)
                pe.wait_ge(added, item + 1)
                for h in range(HEADS):
                    last = pe.matmul(mix_ps[:, h * F1:(h + 1) * F1], agg[:, :, h], wg[:, h, :], start=True, stop=True)
                last.then_inc(mixed, 1)
            window_loop(pe, c.passes[1], body, after)


def gated_update(nc, c, d, sem, out):
    loaded, chain_sem, stored = sem("gr_loaded"), sem("gr_chain"), sem("gr_stored")
    w_turned, w_copied, scaled, turned, copied, mixed, gates_taken = (
        sem(f"gr_{x}") for x in ("w_turned", "w_copied", "scaled", "turned", "copied", "mixed", "gates_taken"))
    dve_turn, act_turn = sem("gr_dve_turn"), sem("gr_act_turn")
    F1, H3 = FEAT + 1, 3 * FEAT
    full = (N // P) * P
    with nc.Block() as block, ExitStack() as ctx:
        sb, ps, _ = allocators(nc, ctx)
        wih, whh = sb("gr_wih", [H3, P]), sb("gr_whh", [H3, FEAT])
        wih_t, whh_t = sb("gr_wih_t", [P, P]), sb("gr_whh_t", [FEAT, P])
        b_ih, b_hh = sb("gr_bih", [P, H3]), sb("gr_bhh", [P, H3])
        rden = sb("gr_rden", [P, NB, HEADS])
        xs = sb("gr_xs", [P, 2, HEADS, FEAT])
        x_t, h_t = sb("gr_xt", [P, 2, P]), sb("gr_ht", [FEAT, 2, P])
        gates = sb("gr_gates", [P, NB, P])
        w_ps, x_ps, h_ps, g_ps = (ps("gr_wps", [P, 512]), ps("gr_xps", [P, 2, 512]), ps("gr_hps", [FEAT, 2, 512]),
                                  ps("gr_gps", [P, 2, 512]))
        acc = c.acc[:, :, :].rearrange("p b (h f) -> p b h f", f=F1)

        @block.sync
        def _(sp):
            sp.dma_start(wih[:, :], d.W_ih).then_inc(loaded, 16)
            sp.dma_start(whh[:, :], d.W_hh).then_inc(loaded, 16)
            sp.dma_start(b_ih[:, :], broadcast_row(d.b_ih, H3)).then_inc(loaded, 16)
            sp.dma_start(b_hh[:, :], broadcast_row(d.b_hh, H3)).then_inc(loaded, 16)
            sp.wait_ge(dve_turn, 5)
            sp.dma_start(out[0:full, :].rearrange("(b p) f -> p b f", p=P), c.x[:, 0:N // P, :]).then_inc(stored, 16)
            sp.dma_start(out[full:N, :], c.x[0:N - full, NB - 1, :]).then_inc(stored, 16)
            sp.wait_ge(stored, 32)

        @block.tensor
        def _(pe):
            pe.wait_ge(loaded, 64)
            pe.transpose(w_ps[:, 0:H3], wih[:, :], c.ident[0:H3, 0:H3])
            pe.transpose(w_ps[0:FEAT, P:P + H3], whh[:, :], c.ident[0:H3, 0:H3]).then_inc(w_turned, 1)
            pe.wait_ge(w_copied, 1)
            for b in range(NB):
                u = b % 2
                pe.wait_ge(scaled, b + 1)
                if b >= 2:
                    pe.wait_ge(copied, b - 1)
                pe.transpose(x_ps[:, u, 0:P], xs[:, u, :, :].rearrange("p h f -> p (h f)"), c.ident[:, :])
                pe.transpose(h_ps[:, u, 0:P], c.h[:, b, :], c.ident[:, :]).then_inc(turned, 1)
                pe.wait_ge(copied, b + 1)
                if b >= 2:
                    pe.wait_ge(gates_taken, b - 1)
                pe.matmul(g_ps[:, u, 0:P], x_t[:, u, :], wih_t[:, :], start=True, stop=False)
                pe.matmul(g_ps[:, u, 0:P], h_t[:, u, :], whh_t[:, :], start=False, stop=True).then_inc(mixed, 1)

        @block.scalar
        def _(act):
            for b in range(NB):
                u = b % 2
                act.wait_ge(turned, b + 1)
                act.activation(x_t[:, u, :], x_ps[:, u, 0:P], ACT.Copy)
                act.activation(h_t[:, u, :], h_ps[:, u, 0:P], ACT.Copy).then_inc(copied, 1)
            act.wait_ge(dve_turn, 1)
            act.activation(gates[:, :, 0:2 * FEAT], gates[:, :, 0:2 * FEAT], ACT.Sigmoid).then_inc(act_turn, 1)
            act.wait_ge(dve_turn, 2)
            act.activation(gates[:, :, 2 * FEAT:H3], gates[:, :, 2 * FEAT:H3], ACT.Tanh).then_inc(act_turn, 1)
            act.wait_ge(dve_turn, 3)
            act.activation(gates[:, :, H3:P], gates[:, :, H3:P], ACT.Exp).then_inc(act_turn, 1)

        @block.vector
        def _(dve):
            chain = Chain(dve, chain_sem)
            chain(dve.tensor_scalar(rden[:, :, :], acc[:, :, :, FEAT], 1e-30, None, ALU.max))
            chain(dve.reciprocal(rden[:, :, :], rden[:, :, :]))
            dve.wait_ge(w_turned, 1)
            chain(dve.memset(wih_t[:, :], 0.0))
            chain(dve.memset(whh_t[:, :], 0.0))
            chain(dve.tensor_copy(wih_t[:, 0:H3], w_ps[:, 0:H3]))
            chain(dve.tensor_copy(whh_t[:, 0:2 * FEAT], w_ps[0:FEAT, P:P + 2 * FEAT]))
            chain(dve.tensor_copy(whh_t[:, H3:P], w_ps[0:FEAT, P + 2 * FEAT:P + H3]))
            dve.sem_inc(w_copied, 1)
            for b in range(NB + 1):
                if b < NB:
                    if b >= 2:
                        dve.wait_ge(turned, b - 1)
                    dve.tensor_tensor(xs[:, b % 2, :, :], acc[:, b, :, 0:FEAT],
                                      bc(rden[:, b, :].unsqueeze(2), [P, HEADS, FEAT]), ALU.mult).then_inc(scaled, 1)
                if b >= 1:
                    dve.wait_ge(mixed, b)
                    dve.tensor_copy(gates[:, b - 1, :], g_ps[:, (b - 1) % 2, 0:P]).then_inc(gates_taken, 1)
            dve.wait_ge(gates_taken, NB)
            dve.wait_ge(loaded, 64)
            rz, i_n, h_n = gates[:, :, 0:2 * FEAT], gates[:, :, 2 * FEAT:H3], gates[:, :, H3:P]
            r, z = gates[:, :, 0:FEAT], gates[:, :, FEAT:2 * FEAT]

            def row(ap, n):
                return bc(ap.unsqueeze(1), [P, NB, n])

            chain(dve.tensor_tensor(gates[:, :, 0:H3], gates[:, :, 0:H3], row(b_ih[:, :], H3), ALU.add))
            chain(dve.tensor_tensor(rz, rz, row(b_hh[:, 0:2 * FEAT], 2 * FEAT), ALU.add))
            dve.sem_inc(dve_turn, 1)
            chain(dve.tensor_tensor(h_n, h_n, row(b_hh[:, 2 * FEAT:H3], FEAT), ALU.add))
            dve.wait_ge(act_turn, 1)
            chain(dve.tensor_tensor(h_n, h_n, r, ALU.mult))
            chain(dve.tensor_tensor(i_n, i_n, h_n, ALU.add))
            dve.sem_inc(dve_turn, 1)
            dve.wait_ge(act_turn, 2)
            chain(dve.tensor_tensor(h_n, c.h[:, :, :], i_n, ALU.subtract))
            chain(dve.tensor_tensor(h_n, h_n, z, ALU.mult))
            chain(dve.tensor_tensor(i_n, i_n, h_n, ALU.add))
            chain(dve.tensor_scalar(h_n, i_n, 0.0, None, ALU.min))
            dve.sem_inc(dve_turn, 1)
            chain(dve.tensor_scalar(i_n, i_n, 0.0, -1.0, ALU.max, ALU.add))
            chain(dve.tensor_tensor(c.x[:, :, :], c.x[:, :, :], i_n, ALU.add))
            dve.wait_ge(act_turn, 3)
            chain(dve.tensor_tensor(c.x[:, :, :], c.x[:, :, :], h_n, ALU.add))
            dve.sem_inc(dve_turn, 2)


class Names:
    pass


def gnn(nc, ins, out):
    d, c = Names(), Names()
    d.stn1_w, d.stn1_b, d.stn2_w, d.stn2_b, d.stn3_w, d.stn3_b, d.stn4_w, d.stn4_b, d.conv_w, d.conv_b = (
        ins[f"L0_gnn_{name}"] for name in ("stn1_w", "stn1_b", "stn2_w", "stn2_b", "stn3_w", "stn3_b", "stn4_w",
                                           "stn4_b", "conv_w", "conv_b"))
    d.W_gat, d.attn_l, d.attn_r, d.W_ih, d.W_hh, d.b_ih, d.b_hh = (
        ins[f"L1_gnn_{name}"] for name in ("W_gat", "attn_l", "attn_r", "W_ih", "W_hh", "b_ih", "b_hh"))
    d.x, d.src, d.dst, d.attr = ins["x"], ins["src"], ins["dst"], ins["edge_attr_3"]

    def dram(name, shape, dt=F32):
        return nc.dram_tensor(name, shape, dt).ap()

    d.off = [dram(f"off{k}", [NB * NW], I32) for k in range(2)]
    d.rec = dram("rec", [EP + 2 * P, ROW])
    d.rec_dst = dram("rec_dst", [EP, 2])
    d.gat_table, d.rows4 = dram("gat_table", [NP, 40]), dram("rows4", [EP + 2 * P, GW])
    d.best, d.er_max = dram("best", [NP * HEADS]), dram("er_max", [NP, 2 * HEADS])
    d.hid_table, d.feat_table, d.move = dram("hid_table", [NP, HID]), dram("feat_table", [NP, 36]), dram("move", [NP, 4])
    d.rows2, d.rows3 = dram("rows2", [EP + 2 * P, HID + ROW]), dram("rows3", [EP + 2 * P, 36 + ROW])
    with ExitStack() as top:
        sb, ps, sem = allocators(nc, top)
        c.gathered = [sem(f"gathered{u}") for u in range(RING)]
        c.scattered = [sem(f"scattered{u}") for u in range(2)]

        def phase(build, *args):
            own = []

            def phase_sem(name):
                own.append(nc.alloc_semaphore(name=name))
                return own[-1]

            build(nc, c, d, phase_sem, *args)
            nc.all_engine_barrier()
            nc.clear_and_free_semaphores(own)
            nc.all_engine_barrier()

        c.ramp_i, c.part_i = sb("ramp_i", [P, P], I32), sb("part_i", [P, 1], I32)
        c.ramp, c.part = sb("ramp", [P, P]), sb("part", [P, 1])
        c.ramp_bf, c.ident_bf = sb("ramp_bf", [P, P], BF16), sb("ident_bf", [P, P], BF16)
        c.ident, c.before, c.after = sb("ident", [P, P]), sb("before", [P, P]), sb("after", [P, P])
        c.ones, c.zeros = sb("ones", [P, P]), sb("zeros", [P, P], BF16)
        c.x, c.h = sb("x_sb", [P, NB, FEAT]), sb("h", [P, NB, FEAT])
        c.deg, c.rdeg = sb("deg", [P, NB]), sb("rdeg", [P, NB])
        c.pass_count = sb("pass_count", [1, 2], I32)
        c.passes = [c.pass_count[:, k:k + 1] for k in range(2)]
        c.window_ramp, c.first = sb("window_ramp", [P, NQ, G, WN]), sb("first", [P, NB])
        c.jm, c.jp, c.up_floor, c.down_floor = (sb(n, [P, 5]) for n in ("jm", "jp", "up_floor", "down_floor"))
        phase(constants)
        with ExitStack() as edges:
            sb_e, _, _ = allocators(nc, edges)
            c.src_i, c.dst_i, c.key_tmp = (sb_e(n, [P, NT], I32) for n in ("src_i", "dst_i", "key_tmp"))
            c.src = sb_e("src_f", [P, NT + G])
            c.src_lo, c.src_hi = sb_e("src_lo", [P, NT + G], BF16), sb_e("src_hi", [P, NT + G], BF16)
            c.dst_lo, c.dst_hi = sb_e("dst_lo", [P, NT], BF16), sb_e("dst_hi", [P, NT], BF16)
            c.rec = sb_e("rec_sb", [P, NT, ROW])
            c.base, c.scan = sb_e("base", [P, 2, NB]), sb_e("scan", [P, NB])
            phase(load_nodes_and_edges)
            phase(count_and_prefix)
            phase(sort_edges)

        with ExitStack() as nodes:
            sb_n, _, _ = allocators(nc, nodes)
            hid = sb_n("hid", [P, NB, HID])
            phase(conv, "c1", d.rec, 0, 1, HID, d.stn1_w, hid[:, :, :], None)
            phase(conv_to_hidden, "h1", hid[:, :, :], d.stn1_b, d.hid_table)
            phase(gather_rows, 0, "g2", d.hid_table, HID, d.rec, ROW, 1, d.rows2)
            phase(conv, "c2", d.rows2, HID, HID, HID, d.stn2_w, hid[:, :, :], None)
            phase(conv_to_hidden, "h2", hid[:, :, :], d.stn2_b, None)
            phase(move_table, hid)
        phase(gather_rows, 1, "g3", d.feat_table, 36, d.rec, ROW, 1, d.rows3)
        c.sum3 = sb("sum3", [P, NB, FEAT])
        phase(conv, "c3", d.rows3, 36, FEAT, FEAT, d.conv_w, c.sum3[:, :, :], d.move)
        c.elr, c.shift = sb("elr", [P, NB, 2 * HEADS]), sb("shift", [P, 1])
        phase(second_norm)
        phase(gather_rows, 2, "g4", d.gat_table, 40, d.rec_dst, 2, 0, d.rows4)
        phase(attention_max)
        c.acc = sb("acc", [P, NB, HEADS * (FEAT + 1)])
        phase(attention_sum)
        phase(gated_update, out)


def kernel(**inputs):
    import numpy as np
    import concourse.bacc as bacc
    from concourse.bass_utils import run_bass_kernel_spmd

    nc = bacc.Bacc("TRN2", target_bir_lowering=False, num_devices=1)
    arrays, ins = {}, {}
    for name, value in inputs.items():
        a = np.ascontiguousarray(value)
        arrays[f"in_{name}"] = a
        ins[name] = nc.dram_tensor(f"in_{name}", a.shape, mybir.dt.from_np(a.dtype), kind="ExternalInput").ap()
    out = nc.dram_tensor("out", (N, FEAT), F32, kind="ExternalOutput").ap()
    gnn(nc, ins, out)
    result = run_bass_kernel_spmd(nc, [arrays], core_ids=[0])
    return result.results[0]["out"]
```

```python
from contextlib import ExitStack

import concourse.bass as bass
from concourse import mybir

F32 = mybir.dt.float32
BF16 = mybir.dt.bfloat16
I32 = mybir.dt.int32
U32 = mybir.dt.uint32
ALU = mybir.AluOpType
ACT = mybir.ActivationFunctionType
X = mybir.AxisListType.X

P = 128
N = 12500
E = 200000
NB = -(-N // P)
NP = NB * P
NT = 1568
EP = P * NT
LAST = E - (P - 1) * NT
G = 8
NG = NT // G
WN = 4
NW = P // WN
NQ = NW // G
SPREADS = 4
ROW = 8
EPS = 1e-5
FEAT = 32
HID = 64
K = 125
HEADS = 4
BIG = 1e30
BT = 20
BROWS = BT * P
TAIL = BROWS
SLOPE = 0.2
GW = FEAT + HEADS
AT_SPLIT = 6


def bc(ap, shape):
    return ap.to_broadcast(shape)


class Chain:

    def __init__(self, eng, sem):
        self.eng, self.sem, self.n = eng, sem, 0

    def __call__(self, ins):
        self.n += 1
        ins.then_inc(self.sem, 1)
        self.eng.wait_ge(self.sem, self.n)


def allocators(nc, ctx):
    def sb(name, shape, dt=F32):
        return ctx.enter_context(nc.sbuf_tensor(name, shape, dt))

    def ps(name, shape, dt=F32):
        return ctx.enter_context(nc.psum_tensor(name, shape, dt))

    def sem(name):
        return ctx.enter_context(nc.semaphore(name))

    return sb, ps, sem


def constants(nc, c, d, sem):
    ready, chain_sem = sem("const_iota"), sem("const_chain")
    with nc.Block() as block:
        @block.gpsimd
        def _(pool):
            pool.iota(c.ramp_i[:, :], pattern=[[1, P]], base=0, channel_multiplier=0).then_inc(ready, 1)
            pool.iota(c.part_i[:, :], pattern=[[0, 1]], base=0, channel_multiplier=1).then_inc(ready, 1)

        @block.vector
        def _(dve):
            chain = Chain(dve, chain_sem)
            dve.wait_ge(ready, 2)
            chain(dve.tensor_copy(c.ramp[:, :], c.ramp_i[:, :]))
            chain(dve.tensor_copy(c.part[:, :], c.part_i[:, :]))
            chain(dve.tensor_copy(c.ramp_bf[:, :], c.ramp[:, :]))
            chain(dve.tensor_scalar(c.ident[:, :], c.ramp[:, :], c.part[:, 0:1], None, ALU.is_equal))
            chain(dve.tensor_copy(c.ident_bf[:, :], c.ident[:, :]))
            chain(dve.tensor_scalar(c.before[:, :], c.ramp[:, :], c.part[:, 0:1], None, ALU.is_lt))
            chain(dve.tensor_scalar(c.after[:, :], c.ramp[:, :], c.part[:, 0:1], None, ALU.is_gt))
            chain(dve.memset(c.ones[:, :], 1.0))
            chain(dve.tensor_copy(c.window_ramp[:, :, :, :].rearrange("p q g r -> p (q g r)"), c.ramp[:, :]))
            chain(dve.tensor_scalar(c.first[:, :], c.ramp[:, 0:NB], float(P), None, ALU.mult))
            chain(dve.tensor_scalar(c.jm[:, :], c.ramp[:, 0:5], -1.0, None, ALU.add))
            chain(dve.tensor_scalar(c.jp[:, :], c.ramp[:, 0:5], 1.0, None, ALU.add))
            chain(dve.memset(c.up_floor[:, :], 0.0))
            chain(dve.memset(c.up_floor[:, 0:1], BIG))
            chain(dve.memset(c.up_floor[:, 1:2], -BIG))
            chain(dve.memset(c.down_floor[:, :], 0.0))
            chain(dve.memset(c.down_floor[:, 3:4], -BIG))
            chain(dve.memset(c.down_floor[:, 4:5], BIG))
            chain(dve.memset(c.zeros[:, :], 0.0))


def layer_norm_relu(dve, chain, act_turn, act_done, turn, out, x, tmp, stat):
    shape = [P, NB, FEAT]
    mean, var, rstd = stat[:, 0, :], stat[:, 1, :], stat[:, 2, :]
    chain(dve.tensor_reduce(mean, x, X, ALU.add))
    chain(dve.tensor_scalar(mean, mean, 1.0 / FEAT, None, ALU.mult))
    chain(dve.tensor_tensor(out, x, bc(mean.unsqueeze(2), shape), ALU.subtract))
    chain(dve.tensor_tensor(tmp, out, out, ALU.mult))
    chain(dve.tensor_reduce(var, tmp, X, ALU.add))
    chain(dve.tensor_scalar(var, var, 1.0 / FEAT, EPS, ALU.mult, ALU.add))
    dve.sem_inc(act_turn, 1)
    dve.wait_ge(act_done, turn)
    chain(dve.reciprocal(rstd, rstd))
    chain(dve.tensor_tensor(out, out, bc(rstd.unsqueeze(2), shape), ALU.mult))
    chain(dve.tensor_scalar(out, out, 0.0, None, ALU.max))


def node_view(dram, f):
    return dram.rearrange("(b p) f -> p b f", p=P)


def load_nodes_and_edges(nc, c, d, sem):
    cleared, loaded, chain_sem, var_ready, std_ready = (
        sem("in_cleared"), sem("in_loaded"), sem("in_chain"), sem("in_var"), sem("in_std"))
    full = (N // P) * P
    with nc.Block() as block, ExitStack() as ctx:
        sb, _, _ = allocators(nc, ctx)
        tmp, stat = sb("ln_tmp", [P, NB, FEAT]), sb("ln_stat", [P, 3, NB])
        pseudo = sb("pseudo", [P, NT, 3])
        ends = sb("in_ends", [1, 2], I32)
        keys_stored = sem("in_keys_stored")

        @block.sync
        def _(sp):
            sp.wait_ge(cleared, 1)
            sp.dma_start(c.x[:, 0:N // P, :], d.x[0:full, :].rearrange("(b p) f -> p b f", p=P)).then_inc(loaded, 16)
            sp.dma_start(c.x[0:N - full, NB - 1, :], d.x[full:N, :]).then_inc(loaded, 16)
            for a, n in ((c.src_i, d.src), (c.dst_i, d.dst)):
                sp.dma_start(a[0:P - 1, :], n[0:(P - 1) * NT].rearrange("(p t) -> p t", t=NT)).then_inc(loaded, 16)
                sp.dma_start(a[P - 1:P, 0:LAST], n[(P - 1) * NT:E].rearrange("(p t) -> p t", p=1)).then_inc(loaded, 16)
            sp.dma_start(pseudo[0:P - 1, :, :],
                         d.attr[0:(P - 1) * NT, :].rearrange("(p t) k -> p t k", t=NT)).then_inc(loaded, 16)
            sp.dma_start(pseudo[P - 1:P, 0:LAST, :],
                         d.attr[(P - 1) * NT:E, :].rearrange("(p t) k -> p t k", p=1)).then_inc(loaded, 16)
            sp.wait_ge(loaded, 16 * 8)
            sp.dma_start(d.src_key.rearrange("(p t) w -> p t w", t=NT), c.src_i[:, :].bitcast(F32).unsqueeze(2))\
                .then_inc(keys_stored, 16)
            sp.dma_start(d.dst_key[1:EP + 1].rearrange("(p t) -> p t", t=NT), c.dst_i[:, :]).then_inc(keys_stored, 16)
            sp.dma_start(d.dst_key[0:1].rearrange("(a n) -> a n", a=1), ends[:, 0:1]).then_inc(keys_stored, 16)
            sp.dma_start(d.dst_key[EP + 1:EP + 2].rearrange("(a n) -> a n", a=1), ends[:, 1:2])\
                .then_inc(keys_stored, 16)
            sp.wait_ge(keys_stored, 64)

        @block.scalar
        def _(act):
            act.wait_ge(var_ready, 1)
            act.activation(stat[:, 2, :], stat[:, 1, :], ACT.Sqrt).then_inc(std_ready, 1)

        @block.vector
        def _(dve):
            chain = Chain(dve, chain_sem)
            chain(dve.memset(c.x[:, :, :], 0.0))
            chain(dve.memset(ends[:, :], -1))
            chain(dve.memset(c.src_i[:, :], NP - 1))
            chain(dve.memset(c.dst_i[:, :], NP - 1))
            for a in (c.src, c.src_lo, c.src_hi):
                chain(dve.memset(a[:, NT:NT + G], 0.0))
            chain(dve.memset(pseudo[:, :, :], 0.0))
            chain(dve.memset(c.rec[:, :, :], 0.0))
            dve.sem_inc(cleared, 1)
            dve.wait_ge(loaded, 16 * 8)
            for key_i, key, lo, hi in ((c.src_i, c.src, c.src_lo, c.src_hi), (c.dst_i, None, c.dst_lo, c.dst_hi)):
                if key is not None:
                    chain(dve.tensor_copy(key[:, 0:NT], key_i[:, :]))
                chain(dve.tensor_scalar(c.key_tmp[:, :], key_i[:, :], P - 1, None, ALU.bitwise_and))
                chain(dve.tensor_copy(lo[:, 0:NT], c.key_tmp[:, :]))
                chain(dve.tensor_scalar(c.key_tmp[:, :], key_i[:, :], 7, None, ALU.logical_shift_right))
                chain(dve.tensor_copy(hi[:, 0:NT], c.key_tmp[:, :]))
            chain(dve.tensor_copy(c.rec[:, :, 0:1], c.src[:, 0:NT].unsqueeze(2)))
            chain(dve.tensor_copy(c.rec[:, :, 1:2].bitcast(I32), c.dst_i[:, :].unsqueeze(2)))
            chain(dve.tensor_copy(c.rec[:, :, 2:5], pseudo[:, :, :]))
            layer_norm_relu(dve, chain, var_ready, std_ready, 1, c.h[:, :, :], c.x[:, :, :], tmp[:, :, :], stat)


def count_and_prefix(nc, c, d, sem):
    free = sem("cnt_free")
    made = sem("cnt_made")
    counted, chain_sem, pe_ready, pe_chain = sem("cnt_done"), sem("cnt_chain"), sem("cnt_pe"), sem("cnt_pe_turn")
    stored, act_c = sem("cnt_stored"), sem("cnt_sorted")
    with nc.Block() as block, ExitStack() as ctx:
        sb, ps, _ = allocators(nc, ctx)
        lo_hot = [sb(f"cnt_lo{k}", [P, 2, G, P], BF16) for k in range(2)]
        hi_hot = [sb(f"cnt_hi{k}", [P, 2, G, NB], BF16) for k in range(2)]
        count = [ps(f"cnt_ps{k}", [P, 512]) for k in range(2)]
        total = ps("cnt_total", [P, 512])
        within = ps("cnt_within", [P, 512])
        turned = ps("cnt_turned", [P, 512])
        off = sb("cnt_off", [NB, 2, NW], I32)
        starts = [sb(f"cnt_starts{k}", [1, NB * NW], I32) for k in range(2)]
        tot_sb = sb("cnt_tot", [P, 2, NB])
        has, own = sb("cnt_has", [P, NB]), sb("cnt_own", [P, NB])
        block_fill, block_size, over = (sb(f"cnt_{n}", [1, w]) for n, w in
                                        (("block_fill", NB + 1), ("block_size", NB), ("over", P)))
        fill, fullest, full_i = sb("cnt_fill", [1, NB * NW]), sb("cnt_fullest", [1, 2]), sb("cnt_full_i", [1, 1], I32)

        @block.vector
        def _(dve):
            with dve.Fori(0, NG // 2) as i:
                for u in range(2):
                    dve.wait_ge(free, i * 2 + u + 1)
                    for k, (lo, hi) in enumerate(((c.src_lo, c.src_hi), (c.dst_lo, c.dst_hi))):
                        at = bass.ds((i * 2 + u) * G, G)
                        dve.tensor_tensor(lo_hot[k][:, u, :, :], bc(c.ramp_bf[:, :].unsqueeze(1), [P, G, P]),
                                          bc(lo[:, at].unsqueeze(2), [P, G, P]), ALU.is_equal).then_inc(made, 1)
                        dve.tensor_tensor(hi_hot[k][:, u, :, :], bc(c.ramp_bf[:, 0:NB].unsqueeze(1), [P, G, NB]),
                                          bc(hi[:, at].unsqueeze(2), [P, G, NB]), ALU.is_equal).then_inc(made, 1)
            chain = Chain(dve, chain_sem)
            dve.wait_ge(counted, 1)
            chain(dve.tensor_copy(c.deg[:, :], count[0][:, 0:NB]))
            chain(dve.tensor_copy(c.base[:, 1, :], count[1][:, 0:NB]))
            dve.sem_inc(pe_ready, 1)
            chain(dve.tensor_scalar(has[:, :], c.base[:, 1, :], 1.0, None, ALU.min))
            dve.wait_ge(counted, 2)
            for k, cnt in enumerate((c.deg[:, :], c.base[:, 1, :])):
                chain(dve.tensor_copy(tot_sb[:, k, :], total[:, k * P:k * P + NB]))
                chain(dve.tensor_tensor_scan(c.scan[:, :], bc(c.ones[:, 0:1], [P, NB]), tot_sb[:, k, :], 0.0,
                                             ALU.mult, ALU.add))
                chain(dve.tensor_tensor(c.scan[:, :], c.scan[:, :], tot_sb[:, k, :], ALU.subtract))
                chain(dve.tensor_tensor(c.base[:, k, :], c.scan[:, :], within[:, k * P:k * P + NB], ALU.add))
            dve.sem_inc(pe_ready, 1)
            dve.wait_ge(counted, 3)
            for k in range(2):
                first = turned[0:NB, k * P:(k + 1) * P].rearrange("p (w n) -> p w n", n=WN)[:, :, 0]
                chain(dve.tensor_copy(off[:, k, :], first))
            dve.sem_inc(pe_ready, 1)
            chain(dve.tensor_copy(c.scan[:, :], c.base[:, 1, :]))
            chain(dve.tensor_scalar(own[:, :], c.first[:, :], c.part[:, 0:1], float(EP), ALU.add, ALU.add))
            chain(dve.tensor_tensor(c.scan[:, :], c.scan[:, :], own[:, :], ALU.subtract))
            chain(dve.tensor_tensor(c.scan[:, :], c.scan[:, :], has[:, :], ALU.mult))
            chain(dve.tensor_tensor(c.head_at[:, :], c.scan[:, :], own[:, :], ALU.add))
            for k in range(2):
                chain(dve.tensor_copy(c.block_start[:, k, :], c.base[0:1, k, :]))
                chain(dve.tensor_copy(block_fill[:, 0:NB], c.base[0:1, k, :]))
                chain(dve.memset(block_fill[:, NB:NB + 1], float(EP)))
                chain(dve.tensor_tensor(block_size[:, :], block_fill[:, 1:NB + 1], block_fill[:, 0:NB], ALU.subtract))
                chain(dve.tensor_reduce(fullest[:, 0:1], block_size[:, :], X, ALU.max))
                chain(dve.tensor_scalar(over[:, :], c.ramp[0:1, :], float(BROWS), fullest[:, 0:1], ALU.mult,
                                        ALU.is_lt))
                chain(dve.tensor_reduce(fullest[:, 1:2], over[:, :], X, ALU.add))
                chain(dve.tensor_copy(c.block_passes[:, k:k + 1], fullest[:, 1:2]))
            dve.wait_ge(act_c, 1)
            for k in range(2):
                last = N // WN
                chain(dve.tensor_tensor(fill[:, 0:last], starts[k][:, 1:last + 1], starts[k][:, 0:last], ALU.subtract))
                chain(dve.tensor_reduce(fullest[:, 0:1], fill[:, 0:last], X, ALU.max))
                chain(dve.tensor_scalar(fullest[:, 1:2], fullest[:, 0:1], float(P - 1), float(P), ALU.add, ALU.max))
                chain(dve.tensor_copy(full_i[:, :], fullest[:, 1:2]))
                chain(dve.tensor_scalar(c.pass_count[:, k:k + 1], full_i[:, :], 7, None, ALU.logical_shift_right))

        @block.tensor
        def _(pe):
            for k in range(2):
                pe.matmul(count[k][:, 0:NB], c.zeros[:, 0:P], c.zeros[:, 0:NB], start=True, stop=False)\
                    .then_inc(free, 1)
            with pe.Fori(0, NG // 2) as i:
                for u in range(2):
                    pe.wait_ge(made, i * 8 + u * 4 + 4)
                    for k in range(2):
                        for j in range(G):
                            last = pe.matmul(count[k][:, 0:NB], lo_hot[k][:, u, j, :], hi_hot[k][:, u, j, :],
                                             start=False, stop=False, skip_group_check=True)
                    last.then_inc(free, 1)
            for k in range(2):
                last = pe.matmul(count[k][:, 0:NB], c.zeros[:, 0:P], c.zeros[:, 0:NB], start=False, stop=True)
            last.then_inc(counted, 1)
            pe.wait_ge(pe_ready, 1)
            for k, cnt in enumerate((c.deg[:, :], c.base[:, 1, :])):
                pe.matmul(total[:, k * P:k * P + NB], c.ones[:, :], cnt, start=True, stop=True)
                last = pe.matmul(within[:, k * P:k * P + NB], c.after[:, :], cnt, start=True, stop=True)
            last.then_inc(counted, 1)
            pe.wait_ge(pe_ready, 2)
            for k in range(2):
                last = pe.transpose(turned[0:NB, k * P:(k + 1) * P], c.base[:, k, :], c.ident[:, :])
            last.then_inc(counted, 1)

        @block.sync
        def _(sp):
            sp.wait_ge(pe_ready, 3)
            for k in range(2):
                sp.dma_start(d.off[k].rearrange("(b w) -> b w", w=NW), off[:, k, :]).then_inc(stored, 16)
            sp.wait_ge(stored, 32)
            for k in range(2):
                sp.dma_start(starts[k][0:1, :], d.off[k].rearrange("(a w) -> a w", a=1)).then_inc(stored, 16)
            sp.wait_ge(stored, 64)
            sp.sem_inc(act_c, 1)


def sort_edges(nc, c, d, sem):
    hots_made = sem("rk_hots_made")
    turned = sem("rk_turned")
    lo_ready = sem("rk_lo_ready")
    cols_made = sem("rk_cols_made")
    rows_made = sem("rk_rows_made")
    looked = sem("rk_looked")
    updated = sem("rk_updated")
    table_ready = sem("rk_table_ready")
    sums = sem("rk_sums")
    place_made = sem("rk_place_made")
    rec_ready = sem("rk_rec_ready")
    scattered = c.scattered
    pool_turn = sem("rk_pool_turn")
    tail_made = sem("rk_tail_made")
    with nc.Block() as block, ExitStack() as ctx:
        sb, ps, _ = allocators(nc, ctx)
        lo_hot, hi_hot = sb("rk_lo", [P, 2, G, P], BF16), sb("rk_hi", [P, 2, G, NB], BF16)
        lo_t = sb("rk_lo_t", [P, 2, G, P])
        table = sb("rk_table", [P, 2, NB])
        junk, junk_l = sb("rk_junk", [P, 2, G, P], BF16), sb("rk_junk_l", [P, 2, G, NB], BF16)
        in_tile, before = sb("rk_in_tile", [P, 2, G]), sb("rk_before", [P, 2, G])
        place = sb("rk_place", [P, 2, G], U32)
        rec = sb("rk_rec", [P, 2, G, ROW])
        cols = sb("rk_cols", [P, 2, G])
        tail = sb("rk_tail", [P, 2, ROW])
        lo_ps = ps("rk_lo_ps", [P, G, P], BF16)
        rows = ps("rk_rows_ps", [P, 2, G, P])
        look = ps("rk_look_ps", [P, 2, 512])
        run = ps("rk_run_ps", [P, 512])

        @block.vector
        def _(dve):
            def hots(g, u):
                at = bass.ds(g * G, G)
                dve.tensor_tensor(lo_hot[:, u, :, :], bc(c.ramp_bf[:, :].unsqueeze(1), [P, G, P]),
                                  bc(c.src_lo[:, at].unsqueeze(2), [P, G, P]), ALU.is_equal).then_inc(hots_made, 1)
                dve.tensor_tensor(hi_hot[:, u, :, :], bc(c.ramp_bf[:, 0:NB].unsqueeze(1), [P, G, NB]),
                                  bc(c.src_hi[:, at].unsqueeze(2), [P, G, NB]), ALU.is_equal).then_inc(hots_made, 1)

            dve.memset(tail[:, :, :], -1.0).then_inc(tail_made, 1)
            dve.sem_inc(sums, 4)
            dve.sem_inc(place_made, 2)
            hots(0, 0)
            with dve.Fori(0, NG // 2) as i:
                for u in range(2):
                    g = i * 2 + u
                    dve.wait_ge(updated, g * G + 1)
                    hots(g + 1, 1 - u)
                    dve.wait_ge(rows_made, g + 1)
                    dve.wait_ge(place_made, g + 1)
                    for j in range(G):
                        dve.scalar_tensor_tensor(junk[:, u, j, :], rows[:, u, j, :], c.src[:, bass.ds(g * G + j, 1)],
                                                 c.before[:, :], ALU.is_equal, ALU.mult,
                                                 accum_out=in_tile[:, u, j:j + 1]).then_inc(sums, 1)
                        dve.wait_ge(looked, g * G + j + 1)
                        dve.tensor_tensor_reduce(junk_l[:, u, j, :], look[:, j % 2, 0:NB], hi_hot[:, u, j, :], 1.0, 0.0,
                                                 ALU.mult, ALU.add, before[:, u, j:j + 1]).then_inc(sums, 1)
                    dve.wait_ge(sums, (g + 1) * 2 * G + 4)
                    dve.wait_ge(scattered[u], i * (16 * G) + 16)
                    dve.tensor_tensor(place[:, u, :], in_tile[:, u, :], before[:, u, :], ALU.add)\
                        .then_inc(place_made, 1)

        @block.tensor
        def _(pe):
            def turn(g, u):
                pe.wait_ge(hots_made, g * 2 + 2)
                if not (isinstance(g, int) and g == 0):
                    pe.wait_ge(lo_ready, g * 4)
                for j in range(G):
                    last = pe.transpose(lo_ps[:, j, :], lo_hot[:, u, j, :], c.ident_bf[:, :])
                last.then_inc(turned, 1)
                pe.wait_ge(cols_made, g + 1)
                for j in range(G):
                    last = pe.matmul(rows[:, u, j, :], bc(cols[:, u, j:j + 1], [P, P]), c.ident[:, :],
                                     start=True, stop=True)
                last.then_inc(rows_made, 1)

            pe.matmul(run[:, 0:NB], c.ident[:, :], c.base[:, 0, :], start=True, stop=True).then_inc(updated, 1)
            turn(0, 0)
            with pe.Fori(0, NG // 2) as i:
                for u in range(2):
                    g = i * 2 + u
                    for j in range(G):
                        pe.wait_ge(lo_ready, g * 4 + j // 2 + 1)
                        pe.wait_ge(table_ready, g * G + j + 1)
                        pe.wait_ge(sums, g * 2 * G + 2 * j + 2)
                        pe.matmul(look[:, j % 2, 0:NB], lo_t[:, u, j, :], table[:, j % 2, :],
                                  start=True, stop=True).then_inc(looked, 1)
                        pe.matmul(run[:, 0:NB], lo_hot[:, u, j, :], hi_hot[:, u, j, :],
                                  start=False, stop=True, skip_group_check=True).then_inc(updated, 1)
                        if j == 3:
                            turn(g + 1, 1 - u)

        @block.scalar
        def _(act):
            def take_cols(g, u):
                act.activation(cols[:, u, :], c.src[:, bass.ds(g * G, G)], ACT.Copy).then_inc(cols_made, 1)

            def take_lo(u, q):
                act.activation(lo_t[:, u, 2 * q:2 * q + 2, :], lo_ps[:, 2 * q:2 * q + 2, :], ACT.Copy)\
                    .then_inc(lo_ready, 1)

            take_cols(0, 0)
            act.wait_ge(updated, 1)
            act.activation(table[:, 0, :], run[:, 0:NB], ACT.Copy).then_inc(table_ready, 1)
            act.wait_ge(turned, 1)
            for q in range(4):
                take_lo(0, q)
            with act.Fori(0, NG // 2) as i:
                for u in range(2):
                    g = i * 2 + u
                    act.wait_ge(rows_made, g + 1)
                    take_cols(g + 1, 1 - u)
                    act.wait_ge(scattered[u], i * (16 * G) + 16)
                    act.activation(rec[:, u, :, :], c.rec[:, bass.ds(g * G, G), :], ACT.Copy).then_inc(rec_ready, 1)
                    for j in range(G):
                        act.wait_ge(updated, g * G + j + 2)
                        act.activation(table[:, (j + 1) % 2, :], run[:, 0:NB], ACT.Copy).then_inc(table_ready, 1)
                        if j == 4:
                            act.wait_ge(turned, g + 2)
                        if j >= 4:
                            take_lo(1 - u, j - 4)

        @block.gpsimd
        def _(pool):
            pool.wait_ge(tail_made, 1)
            for u in range(2):
                pool.dma_start(d.rec[EP + u * P:EP + (u + 1) * P, :], tail[:, u, :]).then_inc(scattered[u], 16)
            with pool.Fori(0, NG // 2) as i:
                for u in range(2):
                    g = i * 2 + u
                    pool.wait_ge(place_made, g + 3)
                    pool.wait_ge(rec_ready, g + 1)
                    pool.sem_inc(pool_turn, 1)
                    for j in range(G):
                        pool.indirect_dma_start(
                            out=d.rec, out_offset=bass.IndirectOffsetOnAxis(ap=place[:, u, j:j + 1], axis=0),
                            in_=rec[:, u, j, :], in_offset=None).then_inc(scattered[u], 16)
            for u in range(2):
                pool.wait_ge(scattered[u], (NG // 2) * 16 * G + 16)


def gather_rows(nc, c, d, sem, turn, name, table, width, rec, rec_width, index_word, rows, with_record, take=None):
    loaded = [sem(f"{name}_loaded{u}") for u in range(RING)]
    gathered, base = c.gathered, turn * (NG // RING) * 16 * G
    stored = [sem(f"{name}_stored{u}") for u in range(RING)]
    kept = sem(f"{name}_kept")
    sp_turn = sem(f"{name}_sp_turn")
    pool_turn = sem(f"{name}_pool_turn")
    tail_made = sem(f"{name}_tail_made")
    whole = width + (rec_width if with_record else 0)
    parts = rows.shape[0] - EP
    rec_v = rec[0:EP, :].rearrange("(p t) w -> p t w", t=NT)
    rows_v = rows[0:EP, :].rearrange("(p t) w -> p t w", t=NT)
    with nc.Block() as block, ExitStack() as ctx:
        sb, _, _ = allocators(nc, ctx)
        ring = sb(f"{name}_ring", [P, RING, G, whole])
        record = ring[:, :, :, width:whole] if with_record else sb(f"{name}_record", [P, RING, G, rec_width])
        tail = sb(f"{name}_tail", [P, parts // P, whole])

        @block.vector
        def _(dve):
            dve.memset(tail[:, :, :], -1.0).then_inc(tail_made, 1)
            if take is not None:
                store, at, n = take
                with dve.Fori(0, NG // RING) as i:
                    for u in range(RING):
                        dve.wait_ge(gathered[u], (i + 1) * (16 * G) + base)
                        dve.tensor_copy(store[:, bass.ds((i * RING + u) * G, G), :], ring[:, u, :, at:at + n])\
                            .then_inc(kept, 1)

        @block.sync
        def _(sp):
            def load(i, u):
                sp.dma_start(record[:, u, :, :], rec_v[:, bass.ds((i * RING + u) * G, G), :])\
                    .then_inc(loaded[u], 16)

            for u in range(RING):
                load(0, u)
            with sp.Fori(1, NG // RING) as i:
                for u in range(RING):
                    sp.wait_ge(stored[u], i * 16)
                    sp.sem_inc(sp_turn, 1)
                    if take is not None:
                        sp.wait_ge(kept, (i - 1) * RING + u + 1)
                        sp.sem_inc(sp_turn, 1)
                    load(i, u)

        @block.gpsimd
        def _(pool):
            with pool.Fori(0, NG // RING) as i:
                for u in range(RING):
                    pool.wait_ge(loaded[u], i * 16 + 16)
                    pool.sem_inc(pool_turn, 1)
                    for j in range(G):
                        at = record[:, u, j, index_word:index_word + 1].bitcast(U32)
                        pool.indirect_dma_start(
                            out=ring[:, u, j, 0:width], out_offset=None, in_=table,
                            in_offset=bass.IndirectOffsetOnAxis(ap=at, axis=0)).then_inc(gathered[u], 16)

        @block.scalar
        def _(act):
            with act.Fori(0, NG // RING) as i:
                for u in range(RING):
                    act.wait_ge(gathered[u], (i + 1) * (16 * G) + base)
                    act.dma_start(rows_v[:, bass.ds((i * RING + u) * G, G), :], ring[:, u, :, 0:whole])\
                        .then_inc(stored[u], 16)
            act.wait_ge(tail_made, 1)
            act.dma_start(rows[EP:EP + parts, :].rearrange("(p t) w -> p t w", p=P), tail[:, :, :])\
                .then_inc(stored[0], 16)
            for u in range(RING):
                act.wait_ge(stored[u], NG // RING * 16 + (16 if u == 0 else 0))


def window_loop(eng, passes, body, after=None, before=None, end=None):
    n = eng.value_load(passes, min_val=1, max_val=EP // P)
    with eng.Fori(0, n) as o:
        if before is not None:
            before(o)
        with eng.Fori(0, NB) as b:
            for q in range(NQ):
                body(b, o * NB + b, q)
            if after is not None:
                after(b, o * NB + b)
        if end is not None:
            end(o)


def block_loop(eng, passes, body, before=None, end=None):
    n = eng.value_load(passes, min_val=1, max_val=EP // BROWS + 1)
    with eng.Fori(0, n) as o:
        if before is not None:
            before(o)
        with eng.Fori(0, NB // 2) as h:
            for u in range(2):
                body(h * 2 + u, o * (NB // 2) + h, u)
        if end is not None:
            end(o)


class Offsets:

    def __init__(self, sb, sem, name, first, n, count):
        self.first, self.count = first, count
        self.now = sb(f"{name}_off_now", [1, n], I32)
        self.ready = sem(f"{name}_off_ready")
        self.taken = sem(f"{name}_off_taken")

    def load(self, sp):
        sp.dma_start(self.now[0:1, :], self.first).then_inc(self.ready, 16)

    def next_pass(self, sp, o):
        sp.wait_ge(self.ready, o + 16)
        sp.sem_inc(self.taken, 1)

    def step(self, dve, o):
        dve.wait_ge(self.ready, o + 16)
        dve.tensor_scalar(self.now[:, :], self.now[:, :], float(self.count), float(EP), ALU.add, ALU.min)\
            .then_inc(self.ready, 1)
        dve.wait_ge(self.ready, o + 17)
        dve.sem_inc(self.taken, 1)


def conv(nc, c, d, sem, name, rows, width, feats, outs, weight, conv_out, moved):
    word = width
    loaded = [sem(f"{name}_loaded{u}") for u in range(NQ)]
    outer_made = sem(f"{name}_outer")
    spread_made = sem(f"{name}_spread")
    dve_seq = sem(f"{name}_dve")
    summed = sem(f"{name}_summed")
    taken = sem(f"{name}_taken")
    batch_done = sem(f"{name}_batch_done")
    mixed = sem(f"{name}_mixed")
    mixed_taken = sem(f"{name}_mixed_taken")
    turned = sem(f"{name}_turned")
    added = sem(f"{name}_added")
    weight_loaded = sem(f"{name}_weight")
    cleared = sem(f"{name}_cleared")
    pair = 2 * WN * feats
    part = G // SPREADS
    with nc.Block() as block, ExitStack() as ctx:
        sb, ps, _ = allocators(nc, ctx)
        rin = sb(f"{name}_rin", [P, NQ, G, width + ROW])
        mark = sb(f"{name}_mark", [P, NQ, G, WN])
        basis = sb(f"{name}_basis_sb", [P, NQ, G, 25, 5])
        spread = sb(f"{name}_spread_sb", [P, NQ, G, WN, feats])
        plane = sb(f"{name}_plane", [P, NQ, G, 5, 5])
        hat = sb(f"{name}_hat", [P, NQ, G, 3, 5])
        rel, pos = sb(f"{name}_rel", [P, G]), sb(f"{name}_pos", [P, G, 3])
        up, down = sb(f"{name}_up", [P, G * 3, 5]), sb(f"{name}_down", [P, G * 3, 5])
        sums = sb(f"{name}_sums", [K, P, feats])
        wsb = sb(f"{name}_w", [K, feats, outs])
        mix_sb = sb(f"{name}_mix_sb", [outs, P])
        offsets = Offsets(sb, sem, name, d.off[0].rearrange("(a w) -> a w", a=1), NB * NW, P)
        acc = [ps(f"{name}_acc{k}", [K, 512]) for k in range(4)]
        mix = ps(f"{name}_mix", [P, 512])
        back = ps(f"{name}_back", [P, 512])
        if moved is not None:
            trow = sb(f"{name}_trow", [P, NQ, G * WN, 4])
            tsel = sb(f"{name}_tsel", [P, G, WN, 3])
            tsrc = sb(f"{name}_tsrc", [P, G, 3])

        @block.sync
        def _(sp):
            offsets.load(sp)
            sp.dma_start(wsb[:, :, :], weight).then_inc(weight_loaded, 16)

            def next_pass(o):
                offsets.next_pass(sp, o)

            def body(b, item, q):
                sp.wait_ge(batch_done, item * NQ + q + 1)
                _, offs = nc.values_load_multi_w_load_instructions(
                    offsets.now[0:1, bass.ds(b * NW + q * G, G)], engines=(sp.engine,), min_val=0, max_val=EP)
                for w in range(G):
                    sp.dma_start(rin[:, q, w, :], rows[bass.ds(offs[w], P), :]).then_inc(loaded[q], 16)
                if moved is not None:
                    sp.dma_start(trow[:, q, :, :].rearrange("p n k -> p (n k)"),
                                 bc(moved[bass.ds(b * P + q * G * WN, G * WN), :].rearrange("n k -> (n k)").unsqueeze(0),
                                    [P, G * WN * 4])).then_inc(loaded[q], 16)
            window_loop(sp, c.passes[0], body, before=next_pass)

        @block.vector
        def _(dve):
            dve.memset(conv_out, 0.0).then_inc(cleared, 1)
            dve.wait_ge(cleared, 1)
            dve.sem_inc(added, 1)
            steps = 9 if moved is None else 13
            loads = 16 * (G if moved is None else G + 1)

            def body(b, item, q):
                m = item * NQ + q

                def after_step(n):
                    dve.wait_ge(dve_seq, m * steps + n)

                def make_spread(k):
                    w = slice(k * part, (k + 1) * part)
                    dve.tensor_tensor(spread[:, q, w, :, :], bc(mark[:, q, w, :].unsqueeze(3), [P, part, WN, feats]),
                                      bc(rin[:, q, w, 0:feats].unsqueeze(2), [P, part, WN, feats]), ALU.mult)\
                        .then_inc(spread_made, 1)

                dve.wait_ge(loaded[q], (item + 1) * loads)
                attr = rin[:, q, :, word + 2:word + 5]
                dve.tensor_scalar(rel[:, :], rin[:, q, :, word], c.first[:, bass.ds(b, 1)], None, ALU.subtract)\
                    .then_inc(dve_seq, 1)
                if moved is None:
                    dve.tensor_copy(pos[:, :, :], attr).then_inc(dve_seq, 1)
                    after_step(1)
                    dve.tensor_tensor(mark[:, q, :, :], bc(rel[:, :].unsqueeze(2), [P, G, WN]),
                                      c.window_ramp[:, q, :, :], ALU.is_equal).then_inc(dve_seq, 1)
                    after_step(2)
                    first = 3
                else:
                    dve.tensor_tensor(pos[:, :, :], attr, rin[:, q, :, feats:feats + 3], ALU.add).then_inc(dve_seq, 1)
                    after_step(1)
                    dve.tensor_tensor(mark[:, q, :, :], bc(rel[:, :].unsqueeze(2), [P, G, WN]),
                                      c.window_ramp[:, q, :, :], ALU.is_equal).then_inc(dve_seq, 1)
                    after_step(3)
                    dve.tensor_tensor(tsel[:, :, :, :].rearrange("p g r k -> p (g r) k"),
                                      bc(mark[:, q, :, :].rearrange("p g r -> p (g r)").unsqueeze(2),
                                         [P, G * WN, 3]), trow[:, q, :, 0:3], ALU.mult).then_inc(dve_seq, 1)
                    make_spread(0)
                    after_step(4)
                    dve.tensor_reduce(tsrc[:, :, :], tsel[:, :, :, :].rearrange("p g r k -> p g k r"), X, ALU.add)\
                        .then_inc(dve_seq, 1)
                    make_spread(1)
                    after_step(5)
                    dve.tensor_tensor(pos[:, :, :], pos[:, :, :], tsrc[:, :, :], ALU.subtract).then_inc(dve_seq, 1)
                    make_spread(2)
                    after_step(6)
                    dve.tensor_scalar(pos[:, :, :], pos[:, :, :], 0.0, 1.0, ALU.max, ALU.min).then_inc(dve_seq, 1)
                    make_spread(3)
                    after_step(7)
                    first = 7
                flat = bc(pos[:, :, :].rearrange("p g k -> p (g k)").unsqueeze(2), [P, G * 3, 5])
                for side, scale, knots, op in ((up, 4.0, c.jm, ALU.subtract), (down, -4.0, c.jp, ALU.add)):
                    dve.scalar_tensor_tensor(side[:, :, :], flat, scale, bc(knots[:, :].unsqueeze(1), [P, G * 3, 5]),
                                             ALU.mult, op).then_inc(dve_seq, 1)
                after_step(first + 1)
                dve.tensor_tensor(up[:, :, :], up[:, :, :], bc(c.up_floor[:, :].unsqueeze(1), [P, G * 3, 5]),
                                  ALU.max).then_inc(dve_seq, 1)
                after_step(first + 2)
                dve.tensor_tensor(down[:, :, :], down[:, :, :], bc(c.down_floor[:, :].unsqueeze(1), [P, G * 3, 5]),
                                  ALU.max).then_inc(dve_seq, 1)
                if moved is None and feats > 1:
                    for k in range(SPREADS // 2):
                        make_spread(k)
                after_step(first + 4)
                dve.tensor_tensor(hat[:, q, :, :, :].rearrange("p g k j -> p (g k) j"), up[:, :, :],
                                  down[:, :, :], ALU.min).then_inc(dve_seq, 1)
                if moved is None and feats > 1:
                    for k in range(SPREADS // 2, SPREADS):
                        make_spread(k)
                after_step(steps - 1)
                dve.tensor_tensor(plane[:, q, :, :, :], bc(hat[:, q, :, 0, :].unsqueeze(3), [P, G, 5, 5]),
                                  bc(hat[:, q, :, 1, :].unsqueeze(2), [P, G, 5, 5]), ALU.mult).then_inc(dve_seq, 1)
                if q == NQ - 1:
                    dve.wait_ge(dve_seq, (m + 1) * steps)

            def step(o):
                offsets.step(dve, o)

            window_loop(dve, c.passes[0], body, end=step)

        @block.gpsimd
        def _(pool):
            steps = 9 if moved is None else 13

            def body(b, item, q):
                pool.wait_ge(dve_seq, (item * NQ + q + 1) * steps)
                pool.tensor_tensor(
                    basis[:, q, :, :, :],
                    bc(plane[:, q, :, :, :].rearrange("p g a b -> p g (a b)").unsqueeze(3), [P, G, 25, 5]),
                    bc(hat[:, q, :, 2, :].unsqueeze(2), [P, G, 25, 5]), ALU.mult).then_inc(outer_made, 1)
            window_loop(pool, c.passes[0], body)

        @block.tensor
        def _(pe):
            pe.wait_ge(weight_loaded, 16)
            pe.matmul(mix[0:1, 0:1], c.zeros[:, 0:1], c.zeros[:, 0:1], start=True, stop=True).then_inc(batch_done, NQ)

            def body(b, item, q):
                pe.wait_ge(outer_made, item * NQ + q + 1)
                if feats > 1:
                    pe.wait_ge(spread_made, (item * NQ + q + 1) * SPREADS)
                for w in range(G):
                    pp = q * (G // 2) + w // 2
                    if w % 2 == 0:
                        pe.wait_ge(taken, item * (NW // 2) + pp + 1)
                    rhs = spread[:, q, w, :, :].rearrange("p n f -> p (n f)") if feats > 1 else mark[:, q, w, :]
                    last = pe.matmul(acc[pp % 4][:, (w % 2) * WN * feats:(w % 2 + 1) * WN * feats],
                                     basis[:, q, w, :, :].rearrange("p a b -> p (a b)"), rhs, start=True, stop=True)
                    if w % 2:
                        last.then_inc(summed, 1)
                pe.wait_ge(summed, item * (NW // 2) + (q + 1) * (G // 2))
                pe.sem_inc(batch_done, 1)

            def after(b, item):
                pe.wait_ge(taken, (item + 1) * (NW // 2) + 4)
                for f in range(feats):
                    last = pe.matmul(mix[0:outs, 0:P], wsb[:, f, :], sums[:, :, f], start=(f == 0), stop=(f == feats - 1))
                last.then_inc(mixed, 1)
                pe.wait_ge(added, item + 1)
                pe.matmul(back[:, 0:outs], c.ident[:, :],
                          conv_out[:, bass.ds(b, 1), :].rearrange("p b o -> p (b o)"), start=True, stop=False)
                pe.wait_ge(mixed_taken, item + 1)
                pe.matmul(back[:, 0:outs], mix_sb[:, :], c.ident[0:outs, 0:outs], start=False, stop=True)\
                    .then_inc(turned, 1)
            window_loop(pe, c.passes[0], body, after)

        @block.scalar
        def _(act):
            act.sem_inc(taken, 4)

            def body(b, item, q):
                for h in range(G // 2):
                    pp = q * (G // 2) + h
                    act.wait_ge(summed, item * (NW // 2) + pp + 1)
                    act.activation(sums[:, pp * 2 * WN:(pp + 1) * 2 * WN, :].rearrange("p n f -> p (n f)"),
                                   acc[pp % 4][:, 0:pair], ACT.Copy).then_inc(taken, 1)

            def after(b, item):
                act.wait_ge(mixed, item + 1)
                act.activation(mix_sb[:, :], mix[0:outs, 0:P], ACT.Copy).then_inc(mixed_taken, 1)
                act.wait_ge(turned, item + 1)
                act.activation(conv_out[:, bass.ds(b, 1), :].rearrange("p b o -> p (b o)"), back[:, 0:outs], ACT.Copy)\
                    .then_inc(added, 1)
            window_loop(act, c.passes[0], body, after)


def broadcast_row(row, n):
    return bc(row.rearrange("(a n) -> a n", a=1), [P, n])


def elu(dve, chain, act_turn, act_done, turn, v, low):
    chain(dve.tensor_scalar(low, v, 0.0, None, ALU.min))
    dve.sem_inc(act_turn, 1)
    dve.wait_ge(act_done, turn)
    chain(dve.scalar_tensor_tensor(v, v, 0.0, low, ALU.max, ALU.add))
    chain(dve.tensor_scalar(v, v, -1.0, None, ALU.add))


def conv_to_hidden(nc, c, d, sem, name, hid, bias_dram, table):
    loaded, chain_sem = sem(f"{name}_loaded"), sem(f"{name}_chain")
    low_ready, exp_ready, stored, made = (sem(f"{name}_{x}") for x in ("low", "exp", "stored", "made"))
    with nc.Block() as block, ExitStack() as ctx:
        sb, _, _ = allocators(nc, ctx)
        low = sb(f"{name}_low_sb", [P, NB, HID])
        bias = sb(f"{name}_bias", [P, HID])

        @block.sync
        def _(sp):
            sp.dma_start(bias[:, :], broadcast_row(bias_dram, HID)).then_inc(loaded, 16)
            if table is not None:
                sp.wait_ge(made, 1)
                sp.dma_start(node_view(table, HID), hid).then_inc(stored, 16)
                sp.wait_ge(stored, 16)

        @block.scalar
        def _(act):
            act.wait_ge(low_ready, 1)
            act.activation(low[:, :, :], low[:, :, :], ACT.Exp).then_inc(exp_ready, 1)

        @block.vector
        def _(dve):
            chain = Chain(dve, chain_sem)
            chain(dve.tensor_scalar(c.rdeg[:, :], c.deg[:, :], 1.0, None, ALU.max))
            chain(dve.reciprocal(c.rdeg[:, :], c.rdeg[:, :]))
            chain(dve.tensor_tensor(hid, hid, bc(c.rdeg[:, :].unsqueeze(2), [P, NB, HID]), ALU.mult))
            dve.wait_ge(loaded, 16)
            chain(dve.tensor_tensor(hid, hid, bc(bias[:, :].unsqueeze(1), [P, NB, HID]), ALU.add))
            elu(dve, chain, low_ready, exp_ready, 1, hid, low[:, :, :])
            dve.sem_inc(made, 1)


RING = 4
SET = 7


def move_table(nc, c, d, sem, hid):
    loaded, chain_sem = sem("mt_loaded"), sem("mt_chain")
    turned, copied, mixed, biased, low_ready, exp_ready, hidden, moved, moved_taken, made, stored = (
        sem(f"mt_{x}") for x in ("turned", "copied", "mixed", "biased", "low", "exp", "hidden", "moved",
                                 "moved_taken", "made", "stored"))
    cols = SET * P
    halves = ((0, 512), (512, cols))
    with nc.Block() as block, ExitStack() as ctx:
        sb, ps, _ = allocators(nc, ctx)
        w3, b3, w4, b4 = sb("w3", [HID, HID]), sb("b3", [HID, 1]), sb("w4", [HID, 3]), sb("b4", [P, 3])
        turned_sb, v, low = sb("mt_t", [HID, cols]), sb("mt_v", [HID, cols]), sb("mt_l", [HID, cols])
        t_all = sb("mt_all", [P, NB, 4])
        table = sb("mt_table", [P, NB, 36])
        turned_ps, mix_ps, t_ps = ps("mt_tp", [HID, 1024]), ps("mt_mp", [HID, 1024]), ps("mt_op", [P, 512])

        @block.sync
        def _(sp):
            sp.dma_start(w3[:, :], d.stn3_w).then_inc(loaded, 16)
            sp.dma_start(b3[:, :], d.stn3_b.rearrange("(o a) -> o a", a=1)).then_inc(loaded, 16)
            sp.dma_start(w4[:, :], d.stn4_w).then_inc(loaded, 16)
            sp.dma_start(b4[:, :], broadcast_row(d.stn4_b, 3)).then_inc(loaded, 16)
            sp.wait_ge(made, 1)
            sp.dma_start(node_view(d.move, 4), t_all[:, :, :]).then_inc(stored, 16)
            sp.dma_start(node_view(d.feat_table, 36), table[:, :, :]).then_inc(stored, 16)
            sp.wait_ge(stored, 32)

        @block.tensor
        def _(pe):
            pe.wait_ge(loaded, 64)
            for s in range(NB // SET):
                if s:
                    pe.wait_ge(copied, s)
                for j in range(SET):
                    last = pe.transpose(turned_ps[:, j * P:(j + 1) * P], hid[:, s * SET + j, :], c.ident[:, :])
                last.then_inc(turned, 1)
                pe.wait_ge(copied, s + 1)
                if s:
                    pe.wait_ge(biased, s)
                for a, z in halves:
                    last = pe.matmul(mix_ps[:, a:z], w3[:, :], turned_sb[:, a:z], start=True, stop=True)
                last.then_inc(mixed, 1)
                pe.wait_ge(hidden, s + 1)
                if s:
                    pe.wait_ge(moved_taken, s)
                for j in range(SET):
                    last = pe.matmul(t_ps[:, 4 * j:4 * j + 3], v[:, j * P:(j + 1) * P], w4[:, :], start=True, stop=True)
                last.then_inc(moved, 1)

        @block.scalar
        def _(act):
            act.wait_ge(loaded, 64)
            for s in range(NB // SET):
                act.wait_ge(turned, s + 1)
                act.activation(turned_sb[:, :], turned_ps[:, 0:cols], ACT.Copy).then_inc(copied, 1)
                act.wait_ge(mixed, s + 1)
                if s:
                    act.wait_ge(moved, s)
                act.activation(v[:, :], mix_ps[:, 0:cols], ACT.Identity, bias=b3[:, 0:1]).then_inc(biased, 1)
                act.wait_ge(low_ready, s + 1)
                act.activation(low[:, :], low[:, :], ACT.Exp).then_inc(exp_ready, 1)

        @block.vector
        def _(dve):
            chain = Chain(dve, chain_sem)
            chain(dve.memset(t_all[:, :, :], 0.0))
            chain(dve.memset(table[:, :, :], 0.0))
            chain(dve.tensor_copy(table[:, :, 0:FEAT], c.h[:, :, :]))
            dve.wait_ge(loaded, 64)
            for s in range(NB // SET):
                dve.wait_ge(biased, s + 1)
                elu(dve, chain, low_ready, exp_ready, s + 1, v[:, :], low[:, :])
                dve.sem_inc(hidden, 1)
                dve.wait_ge(moved, s + 1)
                chain(dve.tensor_tensor(t_all[:, s * SET:(s + 1) * SET, 0:3],
                                        t_ps[:, 0:4 * SET].rearrange("p (j k) -> p j k", k=4)[:, :, 0:3],
                                        bc(b4[:, :].unsqueeze(1), [P, SET, 3]), ALU.add))
                dve.sem_inc(moved_taken, 1)
            chain(dve.tensor_copy(table[:, :, FEAT:FEAT + 3], t_all[:, :, 0:3]))
            dve.sem_inc(made, 1)


def second_norm(nc, c, d, sem):
    loaded, chain_sem, cleared = sem("n2_loaded"), sem("n2_chain"), sem("n2_cleared")
    var_ready, std_ready, weights_ready, normed, turned, copied, scored, scored_taken = (
        sem(f"n2_{x}") for x in ("var", "std", "weights", "normed", "turned", "copied", "scored", "scored_taken"))
    made, stored = sem("n2_made"), sem("n2_stored")
    cols = SET * P
    with nc.Block() as block, ExitStack() as ctx:
        sb, ps, _ = allocators(nc, ctx)
        bias = sb("n2_bias", [P, FEAT])
        wg = sb("n2_wg", [FEAT, HEADS * FEAT])
        attn = sb("n2_attn", [FEAT, 2, HEADS * FEAT])
        prod = sb("n2_prod", [FEAT, 2, HEADS * FEAT])
        score_w = sb("n2_score_w", [FEAT, 2 * HEADS])
        tmp, stat = sb("n2_tmp", [P, NB, FEAT]), sb("n2_stat", [P, 3, NB])
        h_t = sb("n2_ht", [FEAT, cols])
        table = sb("n2_table", [P, NB, GW])
        turned_ps, score_ps = ps("n2_tp", [FEAT, 1024]), ps("n2_sp", [P, 512])

        @block.sync
        def _(sp):
            sp.dma_start(bias[:, :], broadcast_row(d.conv_b, FEAT)).then_inc(loaded, 16)
            sp.dma_start(wg[:, :], d.W_gat).then_inc(loaded, 16)
            for k, a in enumerate((d.attn_l, d.attn_r)):
                sp.dma_start(attn[:, k, :], bc(a.rearrange("(a h) f -> a (h f)", a=1), [FEAT, HEADS * FEAT]))\
                    .then_inc(loaded, 16)
            sp.wait_ge(made, 1)
            sp.dma_start(node_view(d.gat_table, GW), table[:, :, :]).then_inc(stored, 16)
            sp.wait_ge(stored, 16)

        @block.scalar
        def _(act):
            act.wait_ge(var_ready, 1)
            act.activation(stat[:, 2, :], stat[:, 1, :], ACT.Sqrt).then_inc(std_ready, 1)
            for s in range(NB // SET):
                act.wait_ge(turned, s + 1)
                if s:
                    act.wait_ge(scored, s)
                act.activation(h_t[:, :], turned_ps[:, 0:cols], ACT.Copy).then_inc(copied, 1)

        @block.tensor
        def _(pe):
            pe.wait_ge(normed, 1)
            for s in range(NB // SET):
                if s:
                    pe.wait_ge(copied, s)
                for j in range(SET):
                    last = pe.transpose(turned_ps[:, j * P:(j + 1) * P], c.h[:, s * SET + j, :], c.ident[:, :])
                last.then_inc(turned, 1)
                pe.wait_ge(copied, s + 1)
                if s:
                    pe.wait_ge(scored_taken, s)
                for j in range(SET):
                    last = pe.matmul(score_ps[:, 8 * j:8 * j + 8], h_t[:, j * P:(j + 1) * P], score_w[:, :],
                                     start=True, stop=True)
                last.then_inc(scored, 1)

        @block.vector
        def _(dve):
            chain = Chain(dve, chain_sem)
            dve.wait_ge(loaded, 64)
            chain(dve.tensor_tensor(c.sum3[:, :, :], c.sum3[:, :, :], bc(c.rdeg[:, :].unsqueeze(2), [P, NB, FEAT]),
                                    ALU.mult))
            chain(dve.tensor_tensor(c.sum3[:, :, :], c.sum3[:, :, :], bc(bias[:, :].unsqueeze(1), [P, NB, FEAT]),
                                    ALU.add))
            chain(dve.tensor_tensor(c.x[:, :, :], c.x[:, :, :], c.sum3[:, :, :], ALU.add))
            layer_norm_relu(dve, chain, var_ready, std_ready, 1, c.h[:, :, :], c.x[:, :, :], tmp[:, :, :], stat)
            for k in range(2):
                chain(dve.tensor_tensor(prod[:, k, :], wg[:, :], attn[:, k, :], ALU.mult))
            chain(dve.tensor_reduce(score_w[:, :], prod[:, :, :].rearrange("p k (h f) -> p (k h) f", f=FEAT), X,
                                    ALU.add))
            dve.sem_inc(normed, 1)
            chain(dve.tensor_copy(table[:, :, 0:FEAT], c.h[:, :, :]))
            for s in range(NB // SET):
                dve.wait_ge(scored, s + 1)
                chain(dve.tensor_copy(c.elr[:, s * SET:(s + 1) * SET, :],
                                      score_ps[:, 0:8 * SET].rearrange("p (j k) -> p j k", k=8)))
                dve.sem_inc(scored_taken, 1)
            chain(dve.tensor_copy(table[:, :, FEAT:GW], c.elr[:, :, 0:HEADS]))
            dve.sem_inc(made, 1)


def attention_weights(nc, c, d, sem, el):
    loaded, zeroed, zero_stored, chain_sem, act_made = (
        sem(f"aw_{x}") for x in ("loaded", "zeroed", "zero_stored", "chain", "act_made"))
    staged, pool_turn, er_loaded, scattered_all = (
        sem(f"aw_{x}") for x in ("staged", "pool_turn", "er_loaded", "scattered_all"))
    ends_ready, ends_turned, carry_ready, carry_turned = (
        sem(f"aw_{x}") for x in ("ends", "ends_turned", "carry", "carry_turned"))
    exp_ready, exp_done, stored = sem("aw_exp_ready"), sem("aw_exp_done"), sem("aw_stored")
    base = (NG // 2) * 16 * G + 16
    with nc.Block() as block, ExitStack() as ctx:
        sb, ps, _ = allocators(nc, ctx)
        key, near = sb("aw_key", [P, NT], I32), sb("aw_near", [P, NT], I32)
        gap = [sb(f"aw_gap{k}", [P, NT]) for k in range(2)]
        er = sb("aw_er", [P, NT, HEADS])
        out = sb("aw_out", [P, NT, HEADS + 1])
        stage_er, stage_at = sb("aw_stage_er", [P, 2, SET, HEADS]), sb("aw_stage_at", [P, 2, SET], U32)
        tail = sb("aw_tail", [P, BT * (HEADS + 1)])
        turned = sb("aw_turned", [HEADS, 2 * P])
        ends = sb("aw_ends", [P, 2, HEADS])
        row = sb("aw_row", [HEADS, P + 2])
        carry = sb("aw_carry", [P, HEADS])
        ends_ps, carry_ps = ps("aw_ends_ps", [HEADS, 512]), ps("aw_carry_ps", [P, 512])

        @block.sync
        def _(sp):
            sp.dma_start(key[:, :], d.dst_key[1:EP + 1].rearrange("(p t) -> p t", t=NT)).then_inc(loaded, 16)
            sp.dma_start(near[:, :], d.dst_key[0:EP].rearrange("(p t) -> p t", t=NT)).then_inc(loaded, 16)
            sp.wait_ge(zeroed, 1)
            sp.dma_start(d.er_head[0:EP, :].rearrange("(p t) h -> p t h", t=NT), er[:, :, :]).then_inc(zero_stored, 16)
            sp.wait_ge(zeroed, 2)
            sp.dma_start(near[:, :], d.dst_key[2:EP + 2].rearrange("(p t) -> p t", t=NT)).then_inc(loaded, 16)
            sp.wait_ge(scattered_all, 1)
            sp.dma_start(er[:, :, :], d.er_head[0:EP, :].rearrange("(p t) h -> p t h", t=NT)).then_inc(er_loaded, 16)
            sp.wait_ge(zeroed, 3)
            sp.dma_start(d.weights[EP:EP + TAIL, :].rearrange("(p t) w -> p (t w)", p=P), tail[:, :])\
                .then_inc(stored, 16)
            sp.wait_ge(exp_done, 1)
            sp.dma_start(d.weights[0:EP, :].rearrange("(p t) w -> p t w", t=NT), out[:, :, :]).then_inc(stored, 16)
            sp.wait_ge(stored, 32)

        @block.gpsimd
        def _(pool):
            pool.wait_ge(zero_stored, 16)
            with pool.Fori(0, NB // SET // 2) as i:
                for u in range(2):
                    pool.wait_ge(staged, i * 2 + u + 1)
                    pool.sem_inc(pool_turn, 1)
                    for j in range(SET):
                        pool.indirect_dma_start(
                            out=d.er_head, out_offset=bass.IndirectOffsetOnAxis(ap=stage_at[:, u, j:j + 1], axis=0),
                            in_=stage_er[:, u, j, :], in_offset=None).then_inc(c.scattered[u], 16)
            for u in range(2):
                pool.wait_ge(c.scattered[u], base + NB // SET // 2 * SET * 16)
            pool.sem_inc(scattered_all, 1)

        @block.scalar
        def _(act):
            with act.Fori(0, NB // SET // 2) as i:
                for u in range(2):
                    at = bass.ds((i * 2 + u) * SET, SET)
                    act.wait_ge(c.scattered[u], i * (16 * SET) + base)
                    act.activation(stage_er[:, u, :, :], c.elr[:, at, HEADS:2 * HEADS], ACT.Copy)\
                        .then_inc(act_made, 1)
                    act.activation(stage_at[:, u, :], c.head_at[:, at], ACT.Copy).then_inc(act_made, 1)
                    act.wait_ge(act_made, (i * 2 + u) * 2 + 2)
                    act.sem_inc(staged, 1)
            act.wait_ge(exp_ready, 1)
            act.activation(out[:, :, 0:HEADS], out[:, :, 0:HEADS], ACT.Exp).then_inc(exp_done, 1)

        @block.tensor
        def _(pe):
            for n in range(3):
                pe.wait_ge(ends_ready, n + 1)
                for k in range(2):
                    last = pe.transpose(ends_ps[:, k * P:(k + 1) * P], ends[:, k, :], c.ident[:, :])
                last.then_inc(ends_turned, 1)
                pe.wait_ge(carry_ready, n + 1)
                at = 0 if n < 2 else 2
                pe.matmul(carry_ps[:, 0:HEADS], row[:, at:at + P], c.ident[0:HEADS, 0:HEADS], start=True, stop=True)\
                    .then_inc(carry_turned, 1)

        @block.vector
        def _(dve):
            chain = Chain(dve, chain_sem)

            def edge_gap(k):
                chain(dve.tensor_tensor(gap[k][:, :], key[:, :], near[:, :], ALU.is_equal))
                chain(dve.tensor_scalar(gap[k][:, :], gap[k][:, :], -1.0, BIG, ALU.add, ALU.mult))

            def spread_maximum(n, x, y, k):
                def way(ap):
                    return ap if k == 0 else ap[:, ::-1]

                head, last = (0, NT - 1) if k == 0 else (NT - 1, 0)
                for h in range(HEADS):
                    chain(dve.tensor_tensor_scan(way(y[:, :, h]), way(gap[k][:, :]), way(x[:, :, h]), -BIG,
                                                 ALU.add, ALU.max))
                chain(dve.tensor_copy(ends[:, 0, :], y[:, last, 0:HEADS]))
                chain(dve.tensor_reduce(carry[:, 0:1], gap[k][:, :], X, ALU.min))
                chain(dve.tensor_copy(ends[:, 1, :], bc(carry[:, 0:1], [P, HEADS])))
                dve.sem_inc(ends_ready, 1)
                dve.wait_ge(ends_turned, n + 1)
                chain(dve.memset(row[:, :], -BIG))
                chain(dve.tensor_copy(turned[:, :], ends_ps[:, 0:2 * P]))
                chain(dve.tensor_tensor_scan(way(row[:, 1:P + 1]), way(turned[:, P:2 * P]), way(turned[:, 0:P]), -BIG,
                                             ALU.add, ALU.max))
                dve.sem_inc(carry_ready, 1)
                dve.wait_ge(carry_turned, n + 1)
                chain(dve.tensor_scalar(carry[:, :], carry_ps[:, 0:HEADS], gap[k][:, head:head + 1], None, ALU.add))
                chain(dve.tensor_tensor(y[:, head, 0:HEADS], y[:, head, 0:HEADS], carry[:, :], ALU.max))
                for h in range(HEADS):
                    chain(dve.tensor_tensor_scan(way(y[:, :, h]), way(gap[k][:, :]), way(y[:, :, h]), -BIG,
                                                 ALU.add, ALU.max))

            chain(dve.memset(er[:, :, :], -BIG))
            dve.sem_inc(zeroed, 1)
            dve.wait_ge(loaded, 32)
            edge_gap(0)
            dve.sem_inc(zeroed, 1)
            chain(dve.memset(tail[:, :], -1.0))
            dve.sem_inc(zeroed, 1)
            dve.wait_ge(loaded, 48)
            edge_gap(1)
            chain(dve.tensor_copy(out[:, :, HEADS], key[:, :]))
            dve.wait_ge(er_loaded, 16)
            spread_maximum(0, er, er, 0)
            chain(dve.tensor_tensor(el[:, :, :], el[:, :, :], er[:, :, :], ALU.add))
            chain(dve.scalar_tensor_tensor(el[:, :, :], el[:, :, :], SLOPE, el[:, :, :], ALU.mult, ALU.max))
            spread_maximum(1, el, er, 0)
            spread_maximum(2, el, out, 1)
            top = out[:, :, 0:HEADS]
            chain(dve.tensor_tensor(top, top, er[:, :, :], ALU.max))
            chain(dve.tensor_tensor(top, el[:, :, :], top, ALU.subtract))
            dve.sem_inc(exp_ready, 1)


def attention_sum(nc, c, d, sem):
    loaded = [sem(f"at_loaded{u}") for u in range(2)]
    done, seq, mark_made, prod_made, prod_made_pool, agg_done, agg_taken, mixed, added = (
        sem(f"at_{x}") for x in ("done", "seq", "mark_made", "prod_made", "prod_made_pool", "agg_done", "agg_taken", "mixed", "added"))
    w_loaded, cleared, w_cleared = sem("at_w_loaded"), sem("at_cleared"), sem("at_w_cleared")
    with nc.Block() as block, ExitStack() as ctx:
        sb, ps, _ = allocators(nc, ctx)
        rin, win = sb("at_rin", [P, 2, BT, GW]), sb("at_win", [P, 2, BT, HEADS + 1])
        rel = sb("at_rel", [P, BT])
        mark = sb("at_mark", [P, 2, BT, P])
        prod = sb("at_prod", [P, 2, BT, HEADS, FEAT])
        agg = sb("at_agg", [P, 2, P])
        wg = sb("at_wg", [P, P])
        offsets = Offsets(sb, sem, "at", c.block_start[0:1, 1, :], NB, BROWS)
        agg_ps, mix_ps = ps("at_agg_ps", [P, 2, 512]), ps("at_mix_ps", [P, 2, 512])

        @block.sync
        def _(sp):
            offsets.load(sp)
            sp.wait_ge(w_cleared, 1)
            for h in range(HEADS):
                at = slice(h * FEAT, (h + 1) * FEAT)
                sp.dma_start(wg[at, at], d.W_gat[:, at]).then_inc(w_loaded, 16)

            def next_pass(o):
                offsets.next_pass(sp, o)

            def body(b, pair, u):
                sp.wait_ge(done, pair * 2 + u + 1)
                sp.sem_inc(offsets.taken, 1)
                off = sp.value_load(offsets.now[0:1, bass.ds(b, 1)], min_val=0, max_val=EP)
                sp.dma_start(rin[:, u, :, :], d.rows4[bass.ds(off, BROWS), :].rearrange("(p t) w -> p t w", t=BT))\
                    .then_inc(loaded[u], 16)
                sp.dma_start(win[:, u, :, :], d.weights[bass.ds(off, BROWS), :].rearrange("(p t) w -> p t w", t=BT))\
                    .then_inc(loaded[u], 16)
            block_loop(sp, c.block_passes[:, 1:2], body, before=next_pass)

        def products(eng, u, tiles):
            return eng.tensor_tensor(prod[:, u, tiles, :, :],
                                     bc(win[:, u, tiles, 0:HEADS].unsqueeze(3), [P, tiles.stop - tiles.start, HEADS, FEAT]),
                                     bc(rin[:, u, tiles, 0:FEAT].unsqueeze(2), [P, tiles.stop - tiles.start, HEADS, FEAT]),
                                     ALU.mult)

        @block.vector
        def _(dve):
            dve.memset(wg[:, :], 0.0).then_inc(w_cleared, 1)
            dve.memset(c.acc[:, :, :], 0.0).then_inc(cleared, 1)
            dve.wait_ge(cleared, 1)
            dve.sem_inc(added, 2)

            def body(b, pair, u):
                item = pair * 2 + u
                dve.wait_ge(loaded[u], pair * 32 + 32)
                dve.tensor_scalar(rel[:, :], win[:, u, :, HEADS], c.first[:, bass.ds(b, 1)], None, ALU.subtract)\
                    .then_inc(seq, 1)
                products(dve, u, slice(0, AT_SPLIT)).then_inc(prod_made, 1)
                dve.wait_ge(seq, item + 1)
                for t in range(0, BT, BT // 2):
                    w = slice(t, t + BT // 2)
                    last = dve.tensor_tensor(mark[:, u, w, :], bc(rel[:, w].unsqueeze(2), [P, BT // 2, P]),
                                             bc(c.ramp[:, :].unsqueeze(1), [P, BT // 2, P]), ALU.is_equal)
                    last.then_inc(mark_made, 1)
                dve.wait_ge(mark_made, item * 2 + 2)

            block_loop(dve, c.block_passes[:, 1:2], body, end=lambda o: offsets.step(dve, o))

        @block.gpsimd
        def _(pool):
            def body(b, pair, u):
                pool.wait_ge(loaded[u], pair * 32 + 32)
                products(pool, u, slice(AT_SPLIT, BT)).then_inc(prod_made_pool, 1)
            block_loop(pool, c.block_passes[:, 1:2], body)

        @block.tensor
        def _(pe):
            pe.matmul(agg_ps[0:1, 0, 0:1], c.zeros[:, 0:1], c.zeros[:, 0:1], start=True, stop=True).then_inc(done, 2)
            pe.wait_ge(w_loaded, 64)

            def body(b, pair, u):
                item = pair * 2 + u
                pe.wait_ge(added, item + 1)
                pe.matmul(mix_ps[:, u, 0:P + HEADS], c.ident[:, :],
                          c.acc[:, bass.ds(b, 1), :].rearrange("p b f -> p (b f)"), start=True, stop=True)
                pe.wait_ge(prod_made, item + 1)
                pe.wait_ge(prod_made_pool, item + 1)
                for t in range(BT):
                    if t % (BT // 2) == 0:
                        pe.wait_ge(mark_made, item * 2 + t // (BT // 2) + 1)
                    pe.matmul(agg_ps[:, u, 0:P], prod[:, u, t, :, :].rearrange("p h f -> p (h f)"), mark[:, u, t, :],
                              start=(t == 0), stop=(t == BT - 1))
                for t in range(BT):
                    last = pe.matmul(mix_ps[:, u, P:P + HEADS], mark[:, u, t, :], win[:, u, t, 0:HEADS],
                                     start=False, stop=True, skip_group_check=True)
                last.then_inc(agg_done, 1)
                pe.wait_ge(agg_done, item + 1)
                pe.sem_inc(done, 1)
                pe.wait_ge(agg_taken, item + 1)
                pe.matmul(mix_ps[:, u, 0:P], agg[:, u, :], wg[:, :], start=False, stop=True, skip_group_check=True)\
                    .then_inc(mixed, 1)
            block_loop(pe, c.block_passes[:, 1:2], body)

        @block.scalar
        def _(act):
            def body(b, pair, u):
                item = pair * 2 + u
                act.wait_ge(agg_done, item + 1)
                act.activation(agg[:, u, :], agg_ps[:, u, 0:P], ACT.Copy).then_inc(agg_taken, 1)
                act.wait_ge(mixed, item + 1)
                act.activation(c.acc[:, bass.ds(b, 1), :].rearrange("p b f -> p (b f)"), mix_ps[:, u, 0:P + HEADS],
                               ACT.Copy).then_inc(added, 1)
            block_loop(act, c.block_passes[:, 1:2], body)


def gated_update(nc, c, d, sem, out):
    loaded, chain_sem, stored = sem("gr_loaded"), sem("gr_chain"), sem("gr_stored")
    w_turned, w_copied, scaled, turned, copied, mixed, gates_taken = (
        sem(f"gr_{x}") for x in ("w_turned", "w_copied", "scaled", "turned", "copied", "mixed", "gates_taken"))
    dve_turn, act_turn = sem("gr_dve_turn"), sem("gr_act_turn")
    H3 = 3 * FEAT
    full = (N // P) * P
    with nc.Block() as block, ExitStack() as ctx:
        sb, ps, _ = allocators(nc, ctx)
        wih, whh = sb("gr_wih", [H3, P]), sb("gr_whh", [H3, FEAT])
        wih_t, whh_t = sb("gr_wih_t", [P, P]), sb("gr_whh_t", [FEAT, P])
        b_ih, b_hh = sb("gr_bih", [P, H3]), sb("gr_bhh", [P, H3])
        rden = sb("gr_rden", [P, NB, HEADS])
        xs = sb("gr_xs", [P, 2, HEADS, FEAT])
        x_t, h_t = sb("gr_xt", [P, 2, P]), sb("gr_ht", [FEAT, 2, P])
        gates = sb("gr_gates", [P, NB, P])
        w_ps, x_ps, h_ps, g_ps = (ps("gr_wps", [P, 512]), ps("gr_xps", [P, 2, 512]), ps("gr_hps", [FEAT, 2, 512]),
                                  ps("gr_gps", [P, 2, 512]))

        @block.sync
        def _(sp):
            sp.dma_start(wih[:, :], d.W_ih).then_inc(loaded, 16)
            sp.dma_start(whh[:, :], d.W_hh).then_inc(loaded, 16)
            sp.dma_start(b_ih[:, :], broadcast_row(d.b_ih, H3)).then_inc(loaded, 16)
            sp.dma_start(b_hh[:, :], broadcast_row(d.b_hh, H3)).then_inc(loaded, 16)
            sp.wait_ge(dve_turn, 5)
            sp.dma_start(out[0:full, :].rearrange("(b p) f -> p b f", p=P), c.x[:, 0:N // P, :]).then_inc(stored, 16)
            sp.dma_start(out[full:N, :], c.x[0:N - full, NB - 1, :]).then_inc(stored, 16)
            sp.wait_ge(stored, 32)

        @block.tensor
        def _(pe):
            pe.wait_ge(loaded, 64)
            pe.transpose(w_ps[:, 0:H3], wih[:, :], c.ident[0:H3, 0:H3])
            pe.transpose(w_ps[0:FEAT, P:P + H3], whh[:, :], c.ident[0:H3, 0:H3]).then_inc(w_turned, 1)
            pe.wait_ge(w_copied, 1)
            for b in range(NB):
                u = b % 2
                pe.wait_ge(scaled, b + 1)
                if b >= 2:
                    pe.wait_ge(copied, b - 1)
                pe.transpose(x_ps[:, u, 0:P], xs[:, u, :, :].rearrange("p h f -> p (h f)"), c.ident[:, :])
                pe.transpose(h_ps[:, u, 0:P], c.h[:, b, :], c.ident[:, :]).then_inc(turned, 1)
                pe.wait_ge(copied, b + 1)
                if b >= 2:
                    pe.wait_ge(gates_taken, b - 1)
                pe.matmul(g_ps[:, u, 0:P], x_t[:, u, :], wih_t[:, :], start=True, stop=False)
                pe.matmul(g_ps[:, u, 0:P], h_t[:, u, :], whh_t[:, :], start=False, stop=True).then_inc(mixed, 1)

        @block.scalar
        def _(act):
            for b in range(NB):
                u = b % 2
                act.wait_ge(turned, b + 1)
                act.activation(x_t[:, u, :], x_ps[:, u, 0:P], ACT.Copy)
                act.activation(h_t[:, u, :], h_ps[:, u, 0:P], ACT.Copy).then_inc(copied, 1)
            act.wait_ge(dve_turn, 1)
            act.activation(gates[:, :, 0:2 * FEAT], gates[:, :, 0:2 * FEAT], ACT.Sigmoid).then_inc(act_turn, 1)
            act.wait_ge(dve_turn, 2)
            act.activation(gates[:, :, 2 * FEAT:H3], gates[:, :, 2 * FEAT:H3], ACT.Tanh).then_inc(act_turn, 1)
            act.wait_ge(dve_turn, 3)
            act.activation(gates[:, :, H3:P], gates[:, :, H3:P], ACT.Exp).then_inc(act_turn, 1)

        @block.vector
        def _(dve):
            chain = Chain(dve, chain_sem)
            chain(dve.tensor_scalar(rden[:, :, :], c.acc[:, :, P:P + HEADS], 1e-30, None, ALU.max))
            chain(dve.reciprocal(rden[:, :, :], rden[:, :, :]))
            dve.wait_ge(w_turned, 1)
            chain(dve.memset(wih_t[:, :], 0.0))
            chain(dve.memset(whh_t[:, :], 0.0))
            chain(dve.tensor_copy(wih_t[:, 0:H3], w_ps[:, 0:H3]))
            chain(dve.tensor_copy(whh_t[:, 0:2 * FEAT], w_ps[0:FEAT, P:P + 2 * FEAT]))
            chain(dve.tensor_copy(whh_t[:, H3:P], w_ps[0:FEAT, P + 2 * FEAT:P + H3]))
            dve.sem_inc(w_copied, 1)
            for b in range(NB + 1):
                if b < NB:
                    if b >= 2:
                        dve.wait_ge(turned, b - 1)
                    dve.tensor_tensor(xs[:, b % 2, :, :], c.acc[:, b, 0:P].rearrange("p (h f) -> p h f", h=HEADS),
                                      bc(rden[:, b, :].unsqueeze(2), [P, HEADS, FEAT]), ALU.mult).then_inc(scaled, 1)
                if b >= 1:
                    dve.wait_ge(mixed, b)
                    dve.tensor_copy(gates[:, b - 1, :], g_ps[:, (b - 1) % 2, 0:P]).then_inc(gates_taken, 1)
            dve.wait_ge(gates_taken, NB)
            dve.wait_ge(loaded, 64)
            rz, i_n, h_n = gates[:, :, 0:2 * FEAT], gates[:, :, 2 * FEAT:H3], gates[:, :, H3:P]
            r, z = gates[:, :, 0:FEAT], gates[:, :, FEAT:2 * FEAT]

            def row(ap, n):
                return bc(ap.unsqueeze(1), [P, NB, n])

            chain(dve.tensor_tensor(gates[:, :, 0:H3], gates[:, :, 0:H3], row(b_ih[:, :], H3), ALU.add))
            chain(dve.tensor_tensor(rz, rz, row(b_hh[:, 0:2 * FEAT], 2 * FEAT), ALU.add))
            dve.sem_inc(dve_turn, 1)
            chain(dve.tensor_tensor(h_n, h_n, row(b_hh[:, 2 * FEAT:H3], FEAT), ALU.add))
            dve.wait_ge(act_turn, 1)
            chain(dve.tensor_tensor(h_n, h_n, r, ALU.mult))
            chain(dve.tensor_tensor(i_n, i_n, h_n, ALU.add))
            dve.sem_inc(dve_turn, 1)
            dve.wait_ge(act_turn, 2)
            chain(dve.tensor_tensor(h_n, c.h[:, :, :], i_n, ALU.subtract))
            chain(dve.tensor_tensor(h_n, h_n, z, ALU.mult))
            chain(dve.tensor_tensor(i_n, i_n, h_n, ALU.add))
            chain(dve.tensor_scalar(h_n, i_n, 0.0, None, ALU.min))
            dve.sem_inc(dve_turn, 1)
            chain(dve.tensor_scalar(i_n, i_n, 0.0, -1.0, ALU.max, ALU.add))
            chain(dve.tensor_tensor(c.x[:, :, :], c.x[:, :, :], i_n, ALU.add))
            dve.wait_ge(act_turn, 3)
            chain(dve.tensor_tensor(c.x[:, :, :], c.x[:, :, :], h_n, ALU.add))
            dve.sem_inc(dve_turn, 2)


class Names:
    pass


def gnn(nc, ins, out):
    d, c = Names(), Names()
    d.stn1_w, d.stn1_b, d.stn2_w, d.stn2_b, d.stn3_w, d.stn3_b, d.stn4_w, d.stn4_b, d.conv_w, d.conv_b = (
        ins[f"L0_gnn_{name}"] for name in ("stn1_w", "stn1_b", "stn2_w", "stn2_b", "stn3_w", "stn3_b", "stn4_w",
                                           "stn4_b", "conv_w", "conv_b"))
    d.W_gat, d.attn_l, d.attn_r, d.W_ih, d.W_hh, d.b_ih, d.b_hh = (
        ins[f"L1_gnn_{name}"] for name in ("W_gat", "attn_l", "attn_r", "W_ih", "W_hh", "b_ih", "b_hh"))
    d.x, d.src, d.dst, d.attr = ins["x"], ins["src"], ins["dst"], ins["edge_attr_3"]

    def dram(name, shape, dt=F32):
        return nc.dram_tensor(name, shape, dt).ap()

    d.off = [dram(f"off{k}", [NB * NW], I32) for k in range(2)]
    d.rec = dram("rec", [EP + 2 * P, ROW])
    d.src_key, d.dst_key = dram("src_key", [EP, 1]), dram("dst_key", [EP + 2], I32)
    d.gat_table, d.rows4 = dram("gat_table", [NP, GW]), dram("rows4", [EP + TAIL, GW])
    d.er_head, d.weights = dram("er_head", [EP + NP, HEADS]), dram("weights", [EP + TAIL, HEADS + 1])
    d.hid_table, d.feat_table, d.move = dram("hid_table", [NP, HID]), dram("feat_table", [NP, 36]), dram("move", [NP, 4])
    d.rows2, d.rows3 = dram("rows2", [EP + 2 * P, HID + ROW]), dram("rows3", [EP + 2 * P, 36 + ROW])
    with ExitStack() as top:
        sb, ps, sem = allocators(nc, top)
        c.gathered = [sem(f"gathered{u}") for u in range(RING)]
        c.scattered = [sem(f"scattered{u}") for u in range(2)]

        def phase(build, *args):
            own = []

            def phase_sem(name):
                own.append(nc.alloc_semaphore(name=name))
                return own[-1]

            build(nc, c, d, phase_sem, *args)
            nc.all_engine_barrier()
            nc.clear_and_free_semaphores(own)
            nc.all_engine_barrier()

        c.ramp_i, c.part_i = sb("ramp_i", [P, P], I32), sb("part_i", [P, 1], I32)
        c.ramp, c.part = sb("ramp", [P, P]), sb("part", [P, 1])
        c.ramp_bf, c.ident_bf = sb("ramp_bf", [P, P], BF16), sb("ident_bf", [P, P], BF16)
        c.ident, c.before, c.after = sb("ident", [P, P]), sb("before", [P, P]), sb("after", [P, P])
        c.ones, c.zeros = sb("ones", [P, P]), sb("zeros", [P, P], BF16)
        c.x, c.h = sb("x_sb", [P, NB, FEAT]), sb("h", [P, NB, FEAT])
        c.deg, c.rdeg = sb("deg", [P, NB]), sb("rdeg", [P, NB])
        c.pass_count = sb("pass_count", [1, 2], I32)
        c.passes = [c.pass_count[:, k:k + 1] for k in range(2)]
        c.block_start, c.block_passes = sb("block_start", [1, 2, NB], I32), sb("block_passes", [1, 2], I32)
        c.head_at = sb("head_at", [P, NB], U32)
        c.window_ramp, c.first = sb("window_ramp", [P, NQ, G, WN]), sb("first", [P, NB])
        c.jm, c.jp, c.up_floor, c.down_floor = (sb(n, [P, 5]) for n in ("jm", "jp", "up_floor", "down_floor"))
        phase(constants)
        with ExitStack() as edges:
            sb_e, _, _ = allocators(nc, edges)
            c.src_i, c.dst_i, c.key_tmp = (sb_e(n, [P, NT], I32) for n in ("src_i", "dst_i", "key_tmp"))
            c.src = sb_e("src_f", [P, NT + G])
            c.src_lo, c.src_hi = sb_e("src_lo", [P, NT + G], BF16), sb_e("src_hi", [P, NT + G], BF16)
            c.dst_lo, c.dst_hi = sb_e("dst_lo", [P, NT], BF16), sb_e("dst_hi", [P, NT], BF16)
            c.rec = sb_e("rec_sb", [P, NT, ROW])
            c.base, c.scan = sb_e("base", [P, 2, NB]), sb_e("scan", [P, NB])
            phase(load_nodes_and_edges)
            phase(count_and_prefix)
            phase(sort_edges)

        with ExitStack() as nodes:
            sb_n, _, _ = allocators(nc, nodes)
            hid = sb_n("hid", [P, NB, HID])
            phase(conv, "c1", d.rec, 0, 1, HID, d.stn1_w, hid[:, :, :], None)
            phase(conv_to_hidden, "h1", hid[:, :, :], d.stn1_b, d.hid_table)
            phase(gather_rows, 0, "g2", d.hid_table, HID, d.rec, ROW, 1, d.rows2, True)
            phase(conv, "c2", d.rows2, HID, HID, HID, d.stn2_w, hid[:, :, :], None)
            phase(conv_to_hidden, "h2", hid[:, :, :], d.stn2_b, None)
            phase(move_table, hid)
        phase(gather_rows, 1, "g3", d.feat_table, 36, d.rec, ROW, 1, d.rows3, True)
        c.sum3 = sb("sum3", [P, NB, FEAT])
        phase(conv, "c3", d.rows3, 36, FEAT, FEAT, d.conv_w, c.sum3[:, :, :], d.move)
        c.elr = sb("elr", [P, NB, 2 * HEADS])
        phase(second_norm)
        with ExitStack() as attention:
            el = allocators(nc, attention)[0]("el", [P, NT, HEADS])
            phase(gather_rows, 2, "g4", d.gat_table, GW, d.src_key, 1, 0, d.rows4, False, (el, FEAT, HEADS))
            phase(attention_weights, el)
        c.acc = sb("acc", [P, NB, P + HEADS])
        phase(attention_sum)
        phase(gated_update, out)


def kernel(**inputs):
    import numpy as np
    import concourse.bacc as bacc
    from concourse.bass_utils import run_bass_kernel_spmd

    nc = bacc.Bacc("TRN2", target_bir_lowering=False, num_devices=1)
    arrays, ins = {}, {}
    for name, value in inputs.items():
        a = np.ascontiguousarray(value)
        arrays[f"in_{name}"] = a
        ins[name] = nc.dram_tensor(f"in_{name}", a.shape, mybir.dt.from_np(a.dtype), kind="ExternalInput").ap()
    out = nc.dram_tensor("out", (N, FEAT), F32, kind="ExternalOutput").ap()
    gnn(nc, ins, out)
    result = run_bass_kernel_spmd(nc, [arrays], core_ids=[0])
    return result.results[0]["out"]
```
